# Optimizing a Trainium2 kernel written in Bass

```python
import numpy as np
import jax
import jax.numpy as jnp

def _softmax(x, axis=-1):
    return jax.nn.softmax(x, axis=axis)
def _gelu(x):
    return jax.nn.gelu(x, approximate=True)
def _silu(x):
    return jax.nn.silu(x)
def _sigmoid(x):
    return jax.nn.sigmoid(x)
def _layernorm(x, axis=-1, eps=1e-5):
    m = jnp.mean(x, axis=axis, keepdims=True)
    v = jnp.var(x, axis=axis, keepdims=True)
    return (x - m) / jnp.sqrt(v + eps)
def _scatter_add(tgt, idx, src, axis=0):
    return tgt.at[idx].add(src)
def _segment_sum(src, seg, n):
    return jax.ops.segment_sum(src, seg, n)

kernel_name = 'mk_adj_ffn_d1_adj_256_28a5c7'

def setup_inputs(seed: int = 0):
    np.random.seed(seed)
    _w = jnp.asarray
    def _rec_inputs():
        import jax
        import jax.numpy as jnp
        _gk = jax.random.key(seed)
        x = -0.0002928 + 1 * jax.random.normal(jax.random.fold_in(_gk, 1), (128, 128, 256), jnp.float32)
        _w = (1.0 + jnp.arange(128, dtype=jnp.float32)) ** -0.5
        _w = _w / _w.mean()
        _pij = jnp.clip(0.03125 * _w[:, None] * _w[None, :], 0.0, 1.0)
        _a = jax.random.uniform(jax.random.fold_in(_gk, 2), (128, 128, 128)) < _pij
        _a = jnp.logical_or(_a, jnp.swapaxes(_a, -1, -2))
        _a = jnp.logical_or(_a, jnp.eye(128, dtype=bool))
        _af = _a.astype(jnp.float32)
        _af = _af * jax.random.uniform(jax.random.fold_in(_gk, 3), (128, 128, 128), jnp.float32, 0.05, 1)
        adj = _af
        return x, adj
    x, adj = _rec_inputs()
    def _L0_gnn_setup():
        import jax, jax.numpy as jnp
        import numpy as np
        B, N, D, H = (8, 2048, 256, 1024)
        RMS_EPS = 1e-06

        def _rmsnorm(h, w, eps=RMS_EPS):
            var = jnp.mean(jnp.square(h), axis=-1, keepdims=True)
            return h * jax.lax.rsqrt(var + eps) * w
        key = jax.random.key(seed)
        ks = jax.random.split(key, 5)
        x = jax.random.normal(ks[0], (B, N, D), dtype=jnp.float32)
        adjacency = jax.random.uniform(ks[1], (B, N, N), dtype=jnp.float32)
        epsilon = jnp.zeros((), dtype=jnp.float32)
        W1 = jax.random.normal(ks[2], (D, H), dtype=jnp.float32) * (1.0 / np.sqrt(D))
        b1 = jnp.zeros((H,), dtype=jnp.float32)
        rms_weight = jnp.ones((H,), dtype=jnp.float32)
        W2 = jax.random.normal(ks[3], (H, D), dtype=jnp.float32) * (1.0 / np.sqrt(H))
        b2 = jnp.zeros((D,), dtype=jnp.float32)
        return {'x': x, 'adjacency': adjacency, 'epsilon': epsilon, 'W1': W1, 'b1': b1, 'rms_weight': rms_weight, 'W2': W2, 'b2': b2}
    _L0_gnn_all = _L0_gnn_setup()
    _L0_gnn_in = {k: v for k, v in _L0_gnn_all.items() if k in ('epsilon', 'W1', 'b1', 'rms_weight', 'W2', 'b2', )}
    del _L0_gnn_all

    def _L0_ffn_setup():
        import jax, jax.numpy as jnp
        import numpy as np
        NUM_EXPERTS = 8
        TOP_K = 2
        B, S, D = (8, 8192, 256)

        def _moe(tokens, router_w, w1, b1, w2, b2):
            N = tokens.shape[0]
            E = router_w.shape[0]
            logits = tokens.astype(jnp.float32) @ router_w.astype(jnp.float32).T
            probs = jax.nn.softmax(logits, axis=-1)
            rw, re = jax.lax.top_k(probs, TOP_K)
            if TOP_K > 1:
                rw = rw / jnp.maximum(rw.sum(-1, keepdims=True), 1e-12)
            rw = rw.astype(tokens.dtype)
            combine = jnp.zeros((N, E), tokens.dtype).at[jnp.arange(N)[:, None], re].set(rw)
            out = tokens
            for e in range(E):
                h = jax.nn.gelu(tokens @ w1[e] + b1[e], approximate=False)
                y = h @ w2[e] + b2[e]
                out = out + combine[:, e:e + 1] * y
            return out
        key = jax.random.key(seed)
        ks = jax.random.split(key, 4)
        scale = 1.0 / np.sqrt(D).astype(np.float32)
        return {'input_embeddings': jax.random.normal(ks[0], (B, S, D), jnp.float32), 'router_w': jax.random.normal(ks[1], (NUM_EXPERTS, D), jnp.float32) * scale, 'w1': jax.random.normal(ks[2], (NUM_EXPERTS, D, D), jnp.float32) * scale, 'b1': jnp.zeros((NUM_EXPERTS, D), jnp.float32), 'w2': jax.random.normal(ks[3], (NUM_EXPERTS, D, D), jnp.float32) * scale, 'b2': jnp.zeros((NUM_EXPERTS, D), jnp.float32)}
    _L0_ffn_all = _L0_ffn_setup()
    _L0_ffn_in = {k: v for k, v in _L0_ffn_all.items() if k in ('router_w', 'w1', 'b1', 'w2', 'b2', )}
    del _L0_ffn_all

    return {
        "x": x,
        "adj": adj,
        "L0_gnn_epsilon": _L0_gnn_in["epsilon"],
        "L0_gnn_W1": _L0_gnn_in["W1"],
        "L0_gnn_b1": _L0_gnn_in["b1"],
        "L0_gnn_rms_weight": _L0_gnn_in["rms_weight"],
        "L0_gnn_W2": _L0_gnn_in["W2"],
        "L0_gnn_b2": _L0_gnn_in["b2"],
        "L0_ffn_router_w": _L0_ffn_in["router_w"],
        "L0_ffn_w1": _L0_ffn_in["w1"],
        "L0_ffn_b1": _L0_ffn_in["b1"],
        "L0_ffn_w2": _L0_ffn_in["w2"],
        "L0_ffn_b2": _L0_ffn_in["b2"],
    }

def reference(x, adj, L0_gnn_epsilon, L0_gnn_W1, L0_gnn_b1, L0_gnn_rms_weight, L0_gnn_W2, L0_gnn_b2, L0_ffn_router_w, L0_ffn_w1, L0_ffn_b1, L0_ffn_w2, L0_ffn_b2):
    import jax
    import jax.numpy as jnp
    def _L0_gnn_ref(x, adjacency, epsilon, W1, b1, rms_weight, W2, b2):
        import jax, jax.numpy as jnp
        import numpy as np
        B, N, D, H = (8, 2048, 256, 1024)
        RMS_EPS = 1e-06

        def _rmsnorm(h, w, eps=RMS_EPS):
            var = jnp.mean(jnp.square(h), axis=-1, keepdims=True)
            return h * jax.lax.rsqrt(var + eps) * w
        neighbor_sum = jnp.einsum('bnm,bmd->bnd', adjacency, x)
        agg = epsilon * x + neighbor_sum
        h = jnp.einsum('bnd,dh->bnh', agg, W1) + b1
        h = jax.nn.silu(_rmsnorm(h, rms_weight))
        out = jnp.einsum('bnh,hd->bnd', h, W2) + b2
        return out

    def _L0_ffn_ref(input_embeddings, router_w, w1, b1, w2, b2):
        import jax, jax.numpy as jnp
        import numpy as np
        NUM_EXPERTS = 8
        TOP_K = 2
        B, S, D = (8, 8192, 256)

        def _moe(tokens, router_w, w1, b1, w2, b2):
            N = tokens.shape[0]
            E = router_w.shape[0]
            logits = tokens.astype(jnp.float32) @ router_w.astype(jnp.float32).T
            probs = jax.nn.softmax(logits, axis=-1)
            rw, re = jax.lax.top_k(probs, TOP_K)
            if TOP_K > 1:
                rw = rw / jnp.maximum(rw.sum(-1, keepdims=True), 1e-12)
            rw = rw.astype(tokens.dtype)
            combine = jnp.zeros((N, E), tokens.dtype).at[jnp.arange(N)[:, None], re].set(rw)
            out = tokens
            for e in range(E):
                h = jax.nn.gelu(tokens @ w1[e] + b1[e], approximate=False)
                y = h @ w2[e] + b2[e]
                out = out + combine[:, e:e + 1] * y
            return out
        b, s, d = input_embeddings.shape
        tokens = input_embeddings.reshape(b * s, d)
        return _moe(tokens, router_w, w1, b1, w2, b2).reshape(b, s, d)

    x = x + _L0_gnn_ref(_layernorm(x, axis=-1), adj, L0_gnn_epsilon, L0_gnn_W1, L0_gnn_b1, L0_gnn_rms_weight, L0_gnn_W2, L0_gnn_b2)
    x = x + _L0_ffn_ref(_layernorm(x, axis=-1), L0_ffn_router_w, L0_ffn_w1, L0_ffn_b1, L0_ffn_w2, L0_ffn_b2)
    return x


_drawn_inputs = setup_inputs


def setup_inputs(seed=0):
    import zlib

    import numpy as np

    out = dict(_drawn_inputs(seed))
    spreads = {'L0_gnn_b1': (0.0, 0.1),
     'L0_gnn_rms_weight': (1.0, 0.2),
     'L0_gnn_b2': (0.0, 0.1),
     'L0_ffn_b1': (0.0, 0.356),
     'L0_ffn_b2': (0.0, 0.1)}
    factors = {}
    for name, (base, spread) in spreads.items():
        noise = np.random.default_rng([zlib.crc32(name.encode()), seed]).standard_normal(out[name].shape)
        drawn = base * np.exp(spread * noise) if base else spread * noise
        out[name] = jnp.asarray(drawn.astype(out[name].dtype))
    for name, factor in factors.items():
        out[name] = (out[name] * factor).astype(out[name].dtype)
    return out
```

```python
from contextlib import ExitStack

import concourse.bass as bass
from concourse import mybir


F32 = mybir.dt.float32
F32R = mybir.dt.float32r
U32 = mybir.dt.uint32
ALU = mybir.AluOpType
ACT = mybir.ActivationFunctionType
AX_X = mybir.AxisListType.X

P = 128
LN_EPS = 1e-5
RMS_EPS = 1e-6

def _events(NJ, NE, NT):
    ev = {}
    ev["bank"] = ([("logits", "moe")] + [(f"h{j}", "gnn") for j in range(NJ)]
                  + [("ss", "gnn"), ("combT", "moe"), ("adjT", "next"), ("rms", "gnn"),
                     ("b2_0", "moe"), ("b2_1", "moe"), ("agg0", "next"), ("agg1", "next"),
                     ("xT0", "gnn"), ("xT1", "gnn")])
    ev["hidden"] = [(f"{e}_{f}", "moe") for e in range(NE) for f in range(2)]
    ev["expert"] = [(f"{e}_{y}", "moe") for e in range(NE) for y in range(2)]
    ev["w2"] = [(f"{j}", "gnn") for j in range(NJ)]
    ev["gelu"] = [(f"{e}_{f}", "moe") for e in range(NE) for f in range(2)]
    ev["gelu_hi"] = [(f"{e}_{f}", "moe") for e in range(NE) for f in range(2)]
    ev["h"] = [(f"{j}", "gnn") for j in range(NJ)]
    ev["sq"] = [(f"{j}", "gnn") for j in range(NJ)]
    ev["tanh"] = [(f"{j}", "gnn") for j in range(NJ)]
    ev["act_hi"] = [(f"{j}", "gnn") for j in range(NJ)]
    ev["hi"] = [("xn", "next"), ("adjT", "next"), ("agg0", "next"), ("agg1", "next"),
                ("xT0", "gnn"), ("xT1", "gnn")]
    ev["ln"] = ([(f"a_st{t}", "next") for t in range(NT)] + [(f"a_ag{t}", "next") for t in range(NT)]
                + [("a_var", "next")] + [(f"a_x{t}", "next") for t in range(NT)]
                + [(f"b_st{t}", "gnn") for t in range(NT)] + [(f"b_ag{t}", "gnn") for t in range(NT)]
                + [("b_var", "gnn")] + [(f"b_x{t}", "gnn") for t in range(NT)])
    ev["router"] = ([(n, "moe") for n in ["copy", "max", "shift", "sum", "rsum", "prob"]]
                    + [(f"top{t}", "moe") for t in range(NT)] + [(f"idx{t}", "moe") for t in range(NT)]
                    + [(n, "moe") for n in ["cast", "pair", "floor", "rpair", "w", "m0", "m1", "c0", "c1", "comb", "combT"]])
    ev["lo"] = [("xn", "next"), ("adjT", "next"), ("agg0", "next"), ("agg1", "next"),
                ("xT0", "gnn"), ("xT1", "gnn")]
    ev["adj"] = [("epsI", "next")]
    ev["rms"] = [("ms", "gnn"), ("diag", "gnn")]
    ev["y"] = [(f"{j}", "gnn") for j in range(NJ)]
    ev["silu"] = [(f"{j}", "gnn") for j in range(NJ)]
    ev["act_lo"] = [(f"{j}", "gnn") for j in range(NJ)]
    ev["x2"] = [("0", "gnn"), ("1", "gnn")]
    ev["b2"] = [("0", "moe"), ("1", "moe")]
    ev["acc"] = [(f"{e}_{y}", "moe") for e in range(NE) for y in range(2)]
    ev["pow"] = [("exp", "moe"), ("a", "next"), ("rms", "gnn"), ("b", "gnn")]
    ev["gelu_lo"] = [(f"{e}_{f}", "moe") for e in range(NE) for f in range(2)]
    ev["sumsq"] = [(f"{j}", "gnn") for j in range(1, NJ)]
    ev["xb"] = [("x", "next")]
    ev["acc0"] = [("xn2", "gnn")]
    return ev


def gnn_moe_kernel(nc, x, adj, eps, W1, b1, rms_w, W2, b2, router_w, w1, eb1, w2, eb2, out):
    NB, N, D = x.shape
    H = W1.shape[1]
    NE = router_w.shape[0]
    GB = 4
    T = GB * N
    NG = NB // GB
    NT = T // P
    KC = D // P
    NJ = H // P
    assert (N, D, T, KC) == (P, 256, 512, 2)
    EV = _events(NJ, NE, NT)

    def parts(i):
        return [n for n, on in (("next", -1 <= i < NG - 1), ("gnn", 0 <= i < NG), ("moe", 1 <= i <= NG)) if on]

    def count(sem, what, i):
        names = [n for n, _ in EV[sem]]
        where = names.index(what)
        part = EV[sem][where][1]
        if part not in parts(i):
            assert i < 2
            return 0
        total = 0
        for j in range(-1, i):
            total += sum(p in parts(j) for _, p in EV[sem])
        return total + sum(p in parts(i) for _, p in EV[sem][:where + 1])

    class Step:

        def __init__(self, n, k=None):
            self.n, self.k = n, k

        def back(self, d):
            return Step(self.n - d, self.k)

        def at(self, f):
            if self.k is None:
                return f(self.n)
            slope = f(self.n + 2) - f(self.n)
            assert f(self.n + 4) - f(self.n + 2) == slope
            return f(self.n) + self.k * slope

        def has(self, part):
            return part in parts(self.n)

    with ExitStack() as ctx:
        def sb(name, shape, dt=F32):
            return ctx.enter_context(nc.sbuf_tensor(name, shape, dt))

        W1_hi, W1_lo = sb("W1_hi", [P, KC, H], F32R), sb("W1_lo", [P, KC, H], F32R)
        W2_hi, W2_lo = sb("W2_hi", [P, NJ, D], F32R), sb("W2_lo", [P, NJ, D], F32R)
        w1_hi, w1_lo = sb("w1_hi", [P, NE, KC, D], F32R), sb("w1_lo", [P, NE, KC, D], F32R)
        w2_hi, w2_lo = sb("w2_hi", [P, NE, KC, D], F32R), sb("w2_lo", [P, NE, KC, D], F32R)
        wr = sb("wr", [P, KC, NE])
        wr_hi, wr_lo = sb("wr_hi", [P, KC, NE], F32R), sb("wr_lo", [P, KC, NE], F32R)
        ident = sb("ident", [P, P])
        ones = sb("ones", [P, P])
        neg_half = sb("neg_half", [P, NT])
        e_base = sb("e_base", [P, NT, NE])
        expert_no = sb("expert_no", [P, NE])
        eps_col = sb("eps_col", [P, 1])
        b1_col = sb("b1_col", [P, NJ])
        rms_w_col = sb("rms_w_col", [P, NJ])
        half_w = sb("half_w", [P, NJ])
        b2_row = sb("b2_row", [P, D])
        eb1_col = sb("eb1_col", [P, NE, KC])
        eb2_sb = sb("eb2_sb", [NE, D])
        x_in = sb("x_in", [P, 2, GB, D])
        adj_in = sb("adj_in", [P, GB, N])
        acc = sb("acc", [P, 2, NT, D])
        xn = sb("xn", [P, NT, D])
        xn_hi, xn_lo = sb("xn_hi", [P, GB, D], F32R), sb("xn_lo", [P, GB, D], F32R)
        adjT_hi, adjT_lo = sb("adjT_hi", [P, GB, N], F32R), sb("adjT_lo", [P, GB, N], F32R)
        agg_hi, agg_lo = sb("agg_hi", [P, KC, T], F32R), sb("agg_lo", [P, KC, T], F32R)
        h = sb("h", [P, NJ, T])
        sq = sb("sq", [P, 2, T])
        sumsq = sb("sumsq", [P, T])
        diag = sumsq[:, :].rearrange("p (t n) -> p t n", t=NT)
        silu = sb("silu", [P, 2, T])
        act_hi, act_lo = sb("act_hi", [P, 2, T], F32R), sb("act_lo", [P, 2, T], F32R)
        xT_hi, xT_lo = sb("xT_hi", [P, KC, T], F32R), sb("xT_lo", [P, KC, T], F32R)
        gelu = sb("gelu", [P, 2, T])
        gelu_hi, gelu_lo = sb("gelu_hi", [P, 2, KC, T], F32R), sb("gelu_lo", [P, 2, KC, T], F32R)
        stats = sb("stats", [P, 2, NT, 6])
        mean_var = sb("mean_var", [P, 2, NT, 2])
        var_eps = sb("var_eps", [P, 2, NT])
        rstd = sb("rstd", [P, 2, NT])
        ms_eps = sb("ms_eps", [P, NT])
        rrms = sb("rrms", [P, NT])
        logit = sb("logit", [P, NT, NE])
        top_logit = sb("top_logit", [P, NT])
        shifted = sb("shifted", [P, NT, NE])
        expd = sb("expd", [P, NT, NE])
        rsum = sb("rsum", [P, 2, NT])
        prob = sb("prob", [P, NT, NE])
        top = sb("top", [P, NT, NE])
        top_at = sb("top_at", [P, NT, NE], U32)
        top_at_f = sb("top_at_f", [P, NT, 2])
        pair = sb("pair", [P, 3, NT])
        weight = sb("weight", [P, NT, 2])
        mask = sb("mask", [P, 2, NT, NE])
        wmask = sb("wmask", [P, 2, NT, NE])
        comb = sb("comb", [P, NT, NE])
        combT = sb("combT", [NE, T])

        def bank(name):
            return ctx.enter_context(nc.psum_tensor(name, [P, 512], F32))

        A = [bank("A0"), bank("A1")]
        O = [bank("O0"), bank("O1")]
        HB = [bank("H0"), bank("H1")]
        Y = [bank("Y0"), bank("Y1")]

        BANK_OF = {"logits": 0, **{f"h{j}": (j + 1) % 2 for j in range(NJ)}, "ss": 1, "combT": 0,
                   "adjT": 0, "rms": 1, "b2_0": 0, "b2_1": 0, "agg0": 0, "agg1": 1, "xT0": 0, "xT1": 1}

        S = {name: ctx.enter_context(nc.semaphore(f"s_{name}")) for name in EV}
        s_x = [ctx.enter_context(nc.semaphore(f"s_x{p}")) for p in range(2)]
        s_adj = ctx.enter_context(nc.semaphore("s_adj_in"))
        s_out = [ctx.enter_context(nc.semaphore(f"s_out{p}")) for p in range(2)]
        s_small = ctx.enter_context(nc.semaphore("s_small"))
        s_const = ctx.enter_context(nc.semaphore("s_const"))
        s_stage = [ctx.enter_context(nc.semaphore(f"s_stage{p}")) for p in range(4)]
        s_whi = ctx.enter_context(nc.semaphore("s_whi"))
        s_wlo = ctx.enter_context(nc.semaphore("s_wlo"))
        s_passed = ctx.enter_context(nc.semaphore("s_passed"))
        s_wr = ctx.enter_context(nc.semaphore("s_wr"))
        s_halfw = ctx.enter_context(nc.semaphore("s_halfw"))

        def wait(eng, sem, what, it):
            v = it.at(lambda i: count(sem, what, i))
            if it.k is None and v <= 0:
                return
            assert it.k is not None or v > 0
            assert count(sem, what, it.n) > 0, (sem, what, it.n)
            eng.wait_ge(S[sem], v)

        def wait_alone(eng, sem, what, it):
            wait(eng, sem, what, it)
            eng.sem_inc(s_passed, 1)

        def loaded(eng, sem, it, g, per=2):
            eng.wait_ge(sem, it.at(lambda i: 16 * (g(i) // per + 1)))

        SMALL = 7
        CONST = 6

        def iterations(eng, body):
            for i in range(-1, 2):
                body(Step(i))
            with eng.Fori(0, (NG - 4) // 2) as k:
                body(Step(2, k))
                body(Step(3, k))
            for i in range(NG - 2, NG + 1):
                body(Step(i))

        W1_stage = acc[:, :, :, :].rearrange("p a t d -> p (a t d)")
        w1_stage = h[:, :, :].rearrange("p j t -> p (j t)")
        STAGES = [
            (W1_stage, W1.rearrange("(k p) h -> p k h", p=P), W1_hi, W1_lo, "p k h -> p (k h)"),
            (w1_stage, w1.rearrange("e (k p) f -> p (e k) f", p=P), w1_hi, w1_lo, "p e k f -> p (e k f)"),
            (W1_stage, W2.rearrange("(j p) d -> p j d", p=P), W2_hi, W2_lo, "p j d -> p (j d)"),
            (w1_stage, w2.rearrange("e (k p) f -> p (e k) f", p=P), w2_hi, w2_lo, "p e k f -> p (e k f)"),
        ]

        block = ctx.enter_context(nc.Block())

        @block.sync
        def _(sp):
            def load_x(it, g, p):
                sp.dma_start(x_in[:, p, :, :], x[bass.ds(g * GB, GB), :, :].rearrange("b n d -> n b d")).then_inc(s_x[p], 16)

            def load_adj(it, g):
                sp.dma_start(adj_in[:, :, :], adj[bass.ds(g * GB, GB), :, :].rearrange("b n m -> n b m")).then_inc(s_adj, 16)

            def store(it, g, p):
                wait(sp, "acc", f"{NE - 1}_1", it)
                sp.dma_start(out[bass.ds(g * GB, GB), :, :].rearrange("b n d -> n b d"), acc[:, p, :, :]).then_inc(s_out[p], 16)

            def stage(n):
                dst, src, _, _, _ = STAGES[n]
                sp.dma_start(dst.rearrange("p (a b) -> p a b", b=src.shape[2]), src).then_inc(s_stage[n], 16)

            stage(0)
            load_x(None, 0, 0)
            load_adj(None, 0)
            load_x(None, 1, 1)
            stage(1)
            sp.wait_ge(s_whi, 1)
            sp.wait_ge(s_wlo, 1)
            stage(2)
            sp.wait_ge(s_whi, 2)
            sp.wait_ge(s_wlo, 2)
            stage(3)
            wait(sp, "lo", "adjT", Step(-1))
            load_adj(None, 1)

            def body(it, g, p):
                wait(sp, "lo", "adjT", it)
                load_adj(it, g)
                wait(sp, "x2", "1", it)
                load_x(it, g, p)
                if it.has("moe"):
                    store(it, g - 3, 1 - p)

            body(Step(0), 2, 0)
            body(Step(1), 3, 1)
            with sp.Fori(0, (NG - 4) // 2) as k:
                body(Step(2, k), k * 2 + 4, 0)
                body(Step(3, k), k * 2 + 5, 1)
            for i in range(NG - 2, NG + 1):
                store(Step(i), i - 1, (i - 1) % 2)
            sp.wait_ge(s_out[0], 16 * (NG // 2))
            sp.wait_ge(s_out[1], 16 * (NG // 2))

        @block.gpsimd
        def _(pool):
            pool.memset(ident[:, :], 0.0).then_inc(s_const, 1)
            pool.memset(ones[:, :], 1.0).then_inc(s_const, 1)
            pool.memset(neg_half[:, :], -0.5).then_inc(s_const, 1)
            pool.memset(e_base[:, :, :], 2.718281828459045).then_inc(s_const, 1)
            pool.iota(expert_no[:, :], [[1, NE]], base=0, channel_multiplier=0,
                      allow_small_or_imprecise_dtypes=True).then_inc(s_const, 1)
            pool.wait_ge(s_const, 1)
            pool.affine_select(out=ident[:, :], in_=ident[:, :], compare_op=ALU.not_equal, fill=1.0, base=0,
                               pattern=[[-1, P]], channel_multiplier=1).then_inc(s_const, 1)
            with nc.allow_non_contiguous_dma(reason="a few small vectors by column"):
                pool.dma_start(b1_col[:, :], b1.rearrange("(j p) -> p j", p=P)).then_inc(s_small, 16)
                pool.dma_start(rms_w_col[:, :], rms_w.rearrange("(j p) -> p j", p=P)).then_inc(s_small, 16)
                pool.dma_start(eb1_col[:, :, :], eb1.rearrange("e (k p) -> p e k", p=P)).then_inc(s_small, 16)
                for kc in range(KC):
                    pool.dma_start(wr[:, kc, :], router_w[:, kc * P:(kc + 1) * P].rearrange("e p -> p e")).then_inc(s_small, 16)
                pool.dma_start(eb2_sb[:, :], eb2).then_inc(s_small, 16)
                pool.dma_start(eps_col[:, :], eps.partition_broadcast(P)).then_inc(s_small, 16)
                pool.dma_start(b2_row[:, :], b2.partition_broadcast(P)).then_inc(s_small, 16)
            pool.wait_ge(s_const, CONST)
            pool.wait_ge(s_small, 16 * (SMALL + 1))

            def body(it):
                prev = it.back(1)
                moe, gnn, nxt = it.has("moe"), it.has("gnn"), it.has("next")
                p = it.n % 2

                def gelu_low(e):
                    for f in range(2):
                        wait(pool, "gelu_hi", f"{e}_{f}", it)
                        if e >= 2:
                            wait(pool, "expert", f"{e - 2}_1", it)
                        elif prev.has("moe"):
                            wait(pool, "expert", f"{NE + e - 2}_1", prev)
                        pool.tensor_tensor(gelu_lo[:, e % 2, f, :], gelu[:, f, :], gelu_hi[:, e % 2, f, :].bitcast(F32),
                                           ALU.subtract).then_inc(S["gelu_lo"], 1)

                def add_square(j):
                    wait(pool, "sq", f"{j}", it)
                    if j == 1:
                        if prev.has("gnn"):
                            wait(pool, "bank", "rms", prev)
                        pool.tensor_tensor(sumsq[:, :], sq[:, 0, :], sq[:, 1, :], ALU.add).then_inc(S["sumsq"], 1)
                    elif j > 1:
                        wait(pool, "sumsq", f"{j - 1}", it)
                        pool.tensor_tensor(sumsq[:, :], sumsq[:, :], sq[:, j % 2, :], ALU.add).then_inc(S["sumsq"], 1)

                if moe:
                    wait(pool, "router", "shift", it)
                    pool.tensor_tensor(expd[:, :, :], e_base[:, :, :], shifted[:, :, :], ALU.pow).then_inc(S["pow"], 1)
                if nxt:
                    wait(pool, "ln", "a_var", it)
                    pool.tensor_tensor(rstd[:, 0, :], var_eps[:, 0, :], neg_half[:, :], ALU.pow).then_inc(S["pow"], 1)
                if gnn:
                    for j in range(NJ // 2):
                        add_square(j)
                if moe:
                    gelu_low(0)
                if gnn:
                    for j in range(NJ // 2, NJ):
                        add_square(j)
                if moe:
                    gelu_low(1)
                if gnn:
                    wait(pool, "rms", "ms", it)
                    pool.tensor_tensor(rrms[:, :], ms_eps[:, :], neg_half[:, :], ALU.pow).then_inc(S["pow"], 1)
                if nxt:
                    wait(pool, "ln", f"a_x{NT - 1}", it)
                    pool.tensor_tensor(x_in[:, 1 - p, :, :], x_in[:, 1 - p, :, :],
                                       b2_row[:, :].unsqueeze(1).broadcast_to([P, GB, D]), ALU.add).then_inc(S["xb"], 1)
                if moe:
                    for e in range(2, 7):
                        gelu_low(e)
                if gnn:
                    wait(pool, "ln", "b_var", it)
                    pool.tensor_tensor(rstd[:, 1, :], var_eps[:, 1, :], neg_half[:, :], ALU.pow).then_inc(S["pow"], 1)
                if moe:
                    gelu_low(7)
                if gnn:
                    wait(pool, "ln", f"b_x{NT - 1}", it)
                    pool.tensor_tensor(acc[:, p, :, :], acc[:, p, :, :], xn[:, :, :], ALU.add).then_inc(S["acc0"], 1)

            iterations(pool, body)

        @block.scalar
        def _(act):
            for n in range(4):
                src, _, hi, _, flat = STAGES[n]
                act.wait_ge(s_stage[n], 16)
                hi_flat = hi[tuple([slice(None)] * len(hi.shape))].rearrange(flat)
                act.activation(hi_flat, src, ACT.Copy).then_inc(s_whi, 1)
            act.wait_ge(s_small, 16 * (SMALL + 1))

            def body(it):
                prev = it.back(1)
                moe, gnn, nxt = it.has("moe"), it.has("gnn"), it.has("next")

                def gelus(e):
                    for f in range(2):
                        wait(act, "hidden", f"{e}_{f}", it)
                        if e >= 1:
                            wait(act, "gelu_lo", f"{e - 1}_{f}", it)
                        elif prev.has("moe"):
                            wait(act, "gelu_lo", f"{NE - 1}_{f}", prev)
                        act.activation(gelu[:, f, :], HB[f][:, :], ACT.Gelu,
                                       bias=eb1_col[:, e, f:f + 1]).then_inc(S["gelu"], 1)

                def gelu_high(e):
                    for f in range(2):
                        wait(act, "gelu", f"{e}_{f}", it)
                        if e >= 2:
                            wait(act, "expert", f"{e - 2}_1", it)
                        elif prev.has("moe"):
                            wait(act, "expert", f"{NE + e - 2}_1", prev)
                        act.activation(gelu_hi[:, e % 2, f, :], gelu[:, f, :], ACT.Copy).then_inc(S["gelu_hi"], 1)

                def hidden_rows(j):
                    wait(act, "bank", f"h{j}", it)
                    if prev.has("gnn"):
                        wait(act, "silu", f"{j}", prev)
                    elif it.n == 0:
                        act.wait_ge(s_whi, 4)
                        act.wait_ge(s_wlo, 4)
                    act.activation(h[:, j, :], A[BANK_OF[f"h{j}"]][:, :], ACT.Identity,
                                   bias=b1_col[:, j:j + 1]).then_inc(S["h"], 1)
                    if j == 2:
                        wait(act, "sumsq", "1", it)
                    elif j > 2:
                        wait(act, "sumsq", f"{j - 2}", it)
                    elif prev.has("gnn"):
                        wait(act, "sumsq", f"{NJ - 2 + j}", prev)
                    act.activation(sq[:, j % 2, :], A[BANK_OF[f"h{j}"]][:, :], ACT.Square,
                                   bias=b1_col[:, j:j + 1]).then_inc(S["sq"], 1)

                def tanh(j):
                    wait(act, "y", f"{j}", it)
                    if j >= 2:
                        wait(act, "act_lo", f"{j - 2}", it)
                    elif prev.has("gnn"):
                        wait(act, "act_lo", f"{NJ + j - 2}", prev)
                    act.activation(silu[:, j % 2, :], h[:, j, :], ACT.Tanh).then_inc(S["tanh"], 1)

                def silu_high(j):
                    wait(act, "silu", f"{j}", it)
                    if j >= 2:
                        wait(act, "w2", f"{j - 2}", it)
                    elif prev.has("gnn"):
                        wait(act, "w2", f"{NJ + j - 2}", prev)
                    act.activation(act_hi[:, j % 2, :], silu[:, j % 2, :], ACT.Copy).then_inc(S["act_hi"], 1)

                def silu_steps(a, b):
                    for j in range(a, b):
                        if j < NJ:
                            tanh(j)
                        if j >= 1:
                            silu_high(j - 1)

                if moe:
                    gelus(0)
                if gnn:
                    for j in range(0, NJ // 2):
                        hidden_rows(j)
                if moe:
                    gelu_high(0)
                    gelus(1)
                if gnn:
                    for j in range(NJ // 2, NJ):
                        hidden_rows(j)
                if moe:
                    gelu_high(1)
                    gelus(2)
                if nxt:
                    wait(act, "ln", f"a_x{NT - 1}", it)
                    if prev.has("next"):
                        wait(act, "bank", "agg1", prev)
                    act.activation(xn_hi[:, :, :], xn[:, :, :], ACT.Copy).then_inc(S["hi"], 1)
                    wait(act, "adj", "epsI", it)
                    act.activation(adjT_hi[:, :, :], adj_in[:, :, :], ACT.Copy).then_inc(S["hi"], 1)
                if moe:
                    gelu_high(2)
                    gelus(3)
                    gelu_high(3)
                    gelus(4)
                if gnn:
                    silu_steps(0, 3)
                if moe:
                    gelu_high(4)
                    gelus(5)
                if gnn:
                    silu_steps(3, 6)
                if moe:
                    gelu_high(5)
                    gelus(6)
                if gnn:
                    silu_steps(6, NJ + 1)
                if moe:
                    gelu_high(6)
                    gelus(7)
                    gelu_high(7)
                if nxt:
                    for c in range(KC):
                        wait(act, "bank", f"agg{c}", it)
                        act.activation(agg_hi[:, c, :], A[BANK_OF[f"agg{c}"]][:, :], ACT.Copy).then_inc(S["hi"], 1)
                if gnn:
                    for c in range(KC):
                        wait(act, "bank", f"xT{c}", it)
                        act.activation(xT_hi[:, c, :], A[BANK_OF[f"xT{c}"]][:, :], ACT.Copy).then_inc(S["hi"], 1)

            iterations(act, body)

        @block.vector
        def _(dve):
            for n in range(4):
                src, _, hi, lo, flat = STAGES[n]
                dve.wait_ge(s_whi, n + 1)
                ix = tuple([slice(None)] * len(hi.shape))
                dve.tensor_tensor(lo[ix].rearrange(flat), src, hi[ix].rearrange(flat).bitcast(F32),
                                  ALU.subtract).then_inc(s_wlo, 1)
            dve.wait_ge(s_const, CONST)
            dve.wait_ge(s_small, 16 * (SMALL + 1))
            dve.tensor_copy(wr_hi[:, :, :], wr[:, :, :]).then_inc(s_wr, 1)
            dve.wait_ge(s_wr, 1)
            dve.tensor_tensor(wr_lo[:, :, :], wr[:, :, :], wr_hi[:, :, :].bitcast(F32), ALU.subtract).then_inc(s_wr, 1)
            dve.tensor_scalar(half_w[:, :], rms_w_col[:, :], 0.5, None, ALU.mult).then_inc(s_halfw, 1)
            dve.wait_ge(s_halfw, 1)

            def body(it):
                prev = it.back(1)
                moe, gnn, nxt = it.has("moe"), it.has("gnn"), it.has("next")
                p = it.n % 2
                q = 1 - p

                def norm_stats(which, part, src):
                    for t in range(NT):
                        dve.bn_stats(stats[:, part, t, :], src[:, t, :]).then_inc(S["ln"], 1)
                    wait_alone(dve, "ln", f"{which}_st{NT - 1}", it)
                    for t in range(NT):
                        dve.bn_aggr(mean_var[:, part, t, :], stats[:, part, t, :]).then_inc(S["ln"], 1)
                    wait(dve, "ln", f"{which}_ag{NT - 1}", it)
                    dve.tensor_scalar(var_eps[:, part, :], mean_var[:, part, :, 1], LN_EPS, None,
                                      ALU.add).then_inc(S["ln"], 1)

                def norm_apply(which, part, src):
                    wait(dve, "pow", which, it)
                    for t in range(NT):
                        dve.tensor_scalar(xn[:, t, :], src[:, t, :], mean_var[:, part, t, 0:1], rstd[:, part, t:t + 1],
                                          ALU.subtract, ALU.mult).then_inc(S["ln"], 1)

                def router_shift():
                    wait(dve, "bank", "logits", it)
                    dve.tensor_copy(logit[:, :, :], A[0][:, 0:NT * NE].rearrange("p (t e) -> p t e", t=NT)).then_inc(S["router"], 1)
                    wait(dve, "router", "copy", it)
                    dve.tensor_reduce(top_logit[:, :], logit[:, :, :], AX_X, ALU.max).then_inc(S["router"], 1)
                    wait(dve, "router", "max", it)
                    if prev.has("moe"):
                        wait(dve, "pow", "exp", prev)
                    dve.tensor_tensor(shifted[:, :, :], logit[:, :, :], top_logit[:, :].unsqueeze(2).broadcast_to([P, NT, NE]),
                                      ALU.subtract).then_inc(S["router"], 1)

                def router_weights():
                    wait(dve, "pow", "exp", it)
                    dve.tensor_reduce(rsum[:, 0, :], expd[:, :, :], AX_X, ALU.add).then_inc(S["router"], 1)
                    wait(dve, "router", "sum", it)
                    dve.reciprocal(rsum[:, 1, :], rsum[:, 0, :]).then_inc(S["router"], 1)
                    wait(dve, "router", "rsum", it)
                    dve.tensor_tensor(prob[:, :, :], expd[:, :, :], rsum[:, 1, :].unsqueeze(2).broadcast_to([P, NT, NE]),
                                      ALU.mult).then_inc(S["router"], 1)
                    wait_alone(dve, "router", "prob", it)
                    for t in range(NT):
                        dve.max(top[:, t, :], prob[:, t, :]).then_inc(S["router"], 1)
                    wait_alone(dve, "router", f"top{NT - 1}", it)
                    for t in range(NT):
                        dve.max_index(top_at[:, t, :], top[:, t, :], prob[:, t, :]).then_inc(S["router"], 1)
                    wait(dve, "router", f"idx{NT - 1}", it)
                    dve.tensor_copy(top_at_f[:, :, :], top_at[:, :, 0:2]).then_inc(S["router"], 1)
                    dve.tensor_tensor(pair[:, 0, :], top[:, :, 0], top[:, :, 1], ALU.add).then_inc(S["router"], 1)
                    wait(dve, "router", "pair", it)
                    dve.tensor_scalar(pair[:, 1, :], pair[:, 0, :], 1e-12, None, ALU.max).then_inc(S["router"], 1)
                    wait(dve, "router", "floor", it)
                    dve.reciprocal(pair[:, 2, :], pair[:, 1, :]).then_inc(S["router"], 1)
                    wait(dve, "router", "rpair", it)
                    dve.tensor_tensor(weight[:, :, :], top[:, :, 0:2], pair[:, 2, :].unsqueeze(2).broadcast_to([P, NT, 2]),
                                      ALU.mult).then_inc(S["router"], 1)
                    for m in range(2):
                        dve.tensor_tensor(mask[:, m, :, :], expert_no[:, :].unsqueeze(1).broadcast_to([P, NT, NE]),
                                          top_at_f[:, :, m:m + 1].broadcast_to([P, NT, NE]), ALU.is_equal).then_inc(S["router"], 1)
                    for m in range(2):
                        wait(dve, "router", f"m{m}", it)
                        dve.tensor_tensor(wmask[:, m, :, :], mask[:, m, :, :], weight[:, :, m:m + 1].broadcast_to([P, NT, NE]),
                                          ALU.mult).then_inc(S["router"], 1)
                    wait(dve, "router", "c1", it)
                    if prev.has("moe"):
                        wait(dve, "bank", "combT", prev)
                        wait(dve, "acc", f"{NE - 1}_1", prev)
                    dve.tensor_tensor(comb[:, :, :], wmask[:, 0, :, :], wmask[:, 1, :, :], ALU.add).then_inc(S["router"], 1)

                def expert_sum(e):
                    if e == 0:
                        wait(dve, "router", "comb", it)
                        wait(dve, "acc0", "xn2", prev)
                    else:
                        wait(dve, "acc", f"{e - 1}_1", it)
                    if e == 3:
                        wait(dve, "b2", "1", it)
                    for y in range(2):
                        wait(dve, "expert", f"{e}_{y}", it)
                        for t in range(2):
                            tt = 2 * y + t
                            last = dve.scalar_tensor_tensor(out=acc[:, q, tt, :], in0=Y[y][:, t * D:(t + 1) * D],
                                                            scalar=comb[:, tt, e:e + 1], in1=acc[:, q, tt, :],
                                                            op0=ALU.mult, op1=ALU.add)
                        last.then_inc(S["acc"], 1)

                def y_row(j):
                    if j == 0:
                        wait(dve, "bank", "rms", it)
                    wait(dve, "h", f"{j}", it)
                    dve.scalar_tensor_tensor(out=h[:, j, :], in0=h[:, j, :], scalar=half_w[:, j:j + 1], in1=A[1][:, :],
                                             op0=ALU.mult, op1=ALU.mult).then_inc(S["y"], 1)

                def silu_row(j):
                    wait(dve, "tanh", f"{j}", it)
                    dve.scalar_tensor_tensor(out=silu[:, j % 2, :], in0=silu[:, j % 2, :], scalar=1.0, in1=h[:, j, :],
                                             op0=ALU.add, op1=ALU.mult).then_inc(S["silu"], 1)

                def silu_low(j):
                    wait(dve, "act_hi", f"{j}", it)
                    dve.tensor_tensor(act_lo[:, j % 2, :], silu[:, j % 2, :], act_hi[:, j % 2, :].bitcast(F32),
                                      ALU.subtract).then_inc(S["act_lo"], 1)

                def silu_steps(a, b):
                    for s in range(a, b):
                        if s < NJ:
                            y_row(s)
                        if 1 <= s <= NJ:
                            silu_row(s - 1)
                        if s >= 2:
                            silu_low(s - 2)

                def low_of_bank(name, lo, hi):
                    wait(dve, "hi", name, it)
                    dve.tensor_tensor(lo, A[BANK_OF[name]][:, :], hi.bitcast(F32), ALU.subtract).then_inc(S["lo"], 1)

                if moe:
                    router_shift()
                if nxt:
                    loaded(dve, s_x[q], it, lambda i: i + 1)
                    norm_stats("a", 0, x_in[:, q])
                if moe:
                    router_weights()
                if nxt:
                    if it.n >= 0:
                        if prev.has("gnn"):
                            wait(dve, "acc0", "xn2", prev)
                    norm_apply("a", 0, x_in[:, q])
                    wait(dve, "hi", "xn", it)
                    dve.tensor_tensor(xn_lo[:, :, :], xn[:, :, :], xn_hi[:, :, :].bitcast(F32), ALU.subtract).then_inc(S["lo"], 1)
                if moe:
                    expert_sum(0)
                if gnn:
                    wait(dve, "bank", "ss", it)
                    dve.tensor_scalar(ms_eps[:, :], A[1][:, 0:NT], 1.0 / H, RMS_EPS, ALU.mult, ALU.add).then_inc(S["rms"], 1)
                if moe:
                    wait(dve, "bank", "combT", it)
                    dve.tensor_copy(combT[:, :], A[0][0:NE, :]).then_inc(S["router"], 1)
                if nxt:
                    wait(dve, "bank", "adjT", it)
                    dve.scalar_tensor_tensor(out=adj_in[:, :, :], in0=ident[:, :].unsqueeze(1).broadcast_to([P, GB, N]),
                                             scalar=eps_col[:, 0:1], in1=A[0][:, :].rearrange("p (b n) -> p b n", b=GB),
                                             op0=ALU.mult, op1=ALU.add).then_inc(S["adj"], 1)
                if gnn:
                    wait(dve, "pow", "rms", it)
                    dve.tensor_tensor(diag, ident[:, :].unsqueeze(1).broadcast_to([P, NT, P]),
                                      rrms[:, :].unsqueeze(2).broadcast_to([P, NT, P]), ALU.mult).then_inc(S["rms"], 1)
                if nxt:
                    wait(dve, "hi", "adjT", it)
                    dve.tensor_tensor(adjT_lo[:, :, :], adj_in[:, :, :], adjT_hi[:, :, :].bitcast(F32), ALU.subtract).then_inc(S["lo"], 1)
                if moe:
                    expert_sum(1)
                    for y in range(2):
                        wait(dve, "bank", f"b2_{y}", it)
                        wait(dve, "acc", "1_1", it)
                        a = acc[:, q, 2 * y:2 * y + 2, :].rearrange("p t d -> p (t d)")
                        dve.tensor_tensor(a, A[BANK_OF[f"b2_{y}"]][:, :], a, ALU.add).then_inc(S["b2"], 1)
                if gnn:
                    silu_steps(0, 3)
                if moe:
                    wait(dve, "b2", "1", it)
                    expert_sum(2)
                if gnn:
                    silu_steps(3, 5)
                if moe:
                    expert_sum(3)
                if gnn:
                    silu_steps(5, 8)
                if moe:
                    expert_sum(4)
                if gnn:
                    silu_steps(8, NJ + 2)
                if moe:
                    expert_sum(5)
                if gnn:
                    wait(dve, "w2", f"{NJ - 1}", it)
                    wait(dve, "xb", "x", prev)
                    if it.n >= 2:
                        dve.wait_ge(s_out[p], it.at(lambda i: 16 * (i // 2)))
                    for y in range(2):
                        dve.tensor_tensor(acc[:, p, 2 * y:2 * y + 2, :].rearrange("p t d -> p (t d)"), O[y][:, :],
                                          x_in[:, p, 2 * y:2 * y + 2, :].rearrange("p t d -> p (t d)"),
                                          ALU.add).then_inc(S["x2"], 1)
                    wait(dve, "x2", "1", it)
                    norm_stats("b", 1, acc[:, p])
                if nxt:
                    for c in range(KC):
                        low_of_bank(f"agg{c}", agg_lo[:, c, :], agg_hi[:, c, :])
                if moe:
                    expert_sum(6)
                if gnn:
                    norm_apply("b", 1, acc[:, p])
                if gnn:
                    for c in range(KC):
                        low_of_bank(f"xT{c}", xT_lo[:, c, :], xT_hi[:, c, :])
                if moe:
                    expert_sum(7)

            iterations(dve, body)

        @block.tensor
        def _(pe):
            pe.wait_ge(s_const, CONST)
            pe.wait_ge(s_small, 16 * (SMALL + 1))
            pe.wait_ge(s_wr, 2)

            def three(dst, hi, lo, m_hi, m_lo, start, stop):
                pe.matmul(dst, hi, m_hi, start=start, stop=False, skip_group_check=True)
                pe.matmul(dst, hi, m_lo, start=False, stop=False, skip_group_check=True)
                return pe.matmul(dst, lo, m_hi, start=False, stop=stop, skip_group_check=True)

            def body(it):
                prev = it.back(1)
                moe, gnn, nxt = it.has("moe"), it.has("gnn"), it.has("next")

                def expert_hidden(e):
                    for f in range(2):
                        if e >= 1:
                            wait(pe, "gelu", f"{e - 1}_{f}", it)
                        elif prev.has("moe"):
                            wait(pe, "gelu", f"{NE - 1}_{f}", prev)
                        if e == 0 and f == 0:
                            wait(pe, "lo", "xT1", prev)
                        for c in range(KC):
                            fs = slice(f * P, (f + 1) * P)
                            mm = three(HB[f][:, :], w1_hi[:, e, c, fs], w1_lo[:, e, c, fs], xT_hi[:, c, :], xT_lo[:, c, :],
                                       c == 0, c == KC - 1)
                        mm.then_inc(S["hidden"], 1)

                def expert_out(e):
                    for f in range(2):
                        wait(pe, "gelu_lo", f"{e}_{f}", it)
                    for y in range(2):
                        if e >= 1:
                            wait(pe, "acc", f"{e - 1}_{y}", it)
                        elif prev.has("moe"):
                            wait(pe, "acc", f"{NE - 1}_{y}", prev)
                        for t in range(2):
                            ts = slice((2 * y + t) * P, (2 * y + t + 1) * P)
                            for f in range(2):
                                mm = three(Y[y][:, t * D:(t + 1) * D], gelu_hi[:, e % 2, f, ts], gelu_lo[:, e % 2, f, ts],
                                           w2_hi[:, e, f, :], w2_lo[:, e, f, :], f == 0, f == 1)
                        mm.then_inc(S["expert"], 1)

                def hidden_rows(j):
                    if j == 0:
                        wait(pe, "lo", "xT1", prev)
                        wait(pe, "lo", "agg1", prev)
                        if it.n == 0:
                            pe.wait_ge(s_wlo, 1)
                    elif j == 1:
                        if moe:
                            wait(pe, "router", "copy", it)
                        else:
                            wait(pe, "lo", "agg0", prev)
                    else:
                        wait(pe, "sq", f"{j - 2}", it)
                    js = slice(j * P, (j + 1) * P)
                    for c in range(KC):
                        mm = three(A[BANK_OF[f"h{j}"]][:, :], W1_hi[:, c, js], W1_lo[:, c, js], agg_hi[:, c, :], agg_lo[:, c, :],
                                   c == 0, c == KC - 1)
                    mm.then_inc(S["bank"], 1)

                def logits():
                    wait(pe, "lo", "xT1", prev)
                    if nxt or prev.has("next"):
                        wait(pe, "lo", "agg1", prev)
                    for t in range(NT):
                        for c in range(KC):
                            ts = slice(t * P, (t + 1) * P)
                            mm = three(A[0][:, t * NE:(t + 1) * NE], xT_hi[:, c, ts], xT_lo[:, c, ts], wr_hi[:, c, :], wr_lo[:, c, :],
                                       c == 0, c == KC - 1)
                    mm.then_inc(S["bank"], 1)

                def sum_squares():
                    wait(pe, "sq", f"{NJ - 2}", it)
                    wait(pe, "sumsq", f"{NJ - 1}", it)
                    for t in range(NT):
                        mm = pe.matmul(A[1][:, t:t + 1], sumsq[:, t * P:(t + 1) * P], ones[:, 0:1], start=True, stop=True)
                    mm.then_inc(S["bank"], 1)

                def comb_transposed():
                    wait(pe, "router", "comb", it)
                    if gnn:
                        wait(pe, "sq", f"{NJ - 1}", it)
                    else:
                        wait(pe, "router", "copy", it)
                    for t in range(NT):
                        mm = pe.matmul(A[0][0:NE, t * P:(t + 1) * P], comb[:, t, :], ident[:, :], start=True, stop=True)
                    mm.then_inc(S["bank"], 1)

                def adj_transposed():
                    loaded(pe, s_adj, it, lambda i: i + 1, per=1)
                    if moe:
                        wait(pe, "router", "combT", it)
                    elif gnn:
                        wait(pe, "sq", f"{NJ - 1}", it)
                    for b in range(GB):
                        mm = pe.transpose(A[0][:, b * P:(b + 1) * P], adj_in[:, b, :], ident[:, :])
                    mm.then_inc(S["bank"], 1)

                def rms_rows():
                    wait(pe, "rms", "diag", it)
                    pe.matmul(A[1][:, :], ones[:, :], sumsq[:, :], start=True,
                              stop=True).then_inc(S["bank"], 1)

                def b2_rows(y):
                    if y == 0:
                        wait(pe, "router", "combT", it)
                        if nxt:
                            wait(pe, "adj", "epsI", it)
                    else:
                        wait(pe, "b2", "0", it)
                    for t in range(2):
                        tt = 2 * y + t
                        mm = pe.matmul(A[0][:, t * D:(t + 1) * D], combT[:, tt * P:(tt + 1) * P], eb2_sb[:, :], start=True, stop=True)
                    mm.then_inc(S["bank"], 1)

                def project(j):
                    wait(pe, "act_lo", f"{j}", it)
                    if j == 0:
                        if prev.has("gnn"):
                            wait(pe, "x2", "1", prev)
                        if it.n == 0:
                            pe.wait_ge(s_wlo, 3)
                    for y in range(2):
                        for t in range(2):
                            ts = slice((2 * y + t) * P, (2 * y + t + 1) * P)
                            mm = three(O[y][:, t * D:(t + 1) * D], act_hi[:, j % 2, ts], act_lo[:, j % 2, ts],
                                       W2_hi[:, j, :], W2_lo[:, j, :], j == 0 and t == 0, j == NJ - 1)
                    mm.then_inc(S["w2"], 1)

                def aggregate():
                    wait(pe, "lo", "xn", it)
                    wait(pe, "lo", "adjT", it)
                    for c in range(KC):
                        if c == 0:
                            if moe:
                                wait(pe, "b2", "1", it)
                        elif gnn:
                            wait(pe, "y", f"{NJ - 1}", it)
                        cs = slice(c * P, (c + 1) * P)
                        for b in range(GB):
                            mm = three(A[c][:, b * P:(b + 1) * P], xn_hi[:, b, cs], xn_lo[:, b, cs], adjT_hi[:, b, :], adjT_lo[:, b, :],
                                       True, True)
                        mm.then_inc(S["bank"], 1)

                def tokens_transposed():
                    for c in range(KC):
                        if nxt:
                            wait(pe, "lo", f"agg{c}", it)
                        elif c == 0:
                            if moe:
                                wait(pe, "b2", "1", it)
                        else:
                            wait(pe, "y", f"{NJ - 1}", it)
                        if c == 0:
                            wait(pe, "ln", f"b_x{NT - 1}", it)
                        for t in range(NT):
                            mm = pe.transpose(A[c][:, t * P:(t + 1) * P], xn[:, t, c * P:(c + 1) * P], ident[:, :])
                        mm.then_inc(S["bank"], 1)

                if moe:
                    logits()
                    if it.n == 1:
                        pe.wait_ge(s_wlo, 4)
                    expert_hidden(0)
                if gnn:
                    for j in range(NJ // 2):
                        hidden_rows(j)
                if moe:
                    expert_hidden(1)
                if gnn:
                    for j in range(NJ // 2, NJ):
                        hidden_rows(j)
                if moe:
                    expert_out(0)
                    expert_hidden(2)
                if gnn:
                    sum_squares()
                if moe:
                    comb_transposed()
                if nxt:
                    adj_transposed()
                if moe:
                    expert_out(1)
                    expert_hidden(3)
                if gnn:
                    rms_rows()
                if moe:
                    b2_rows(0)
                    b2_rows(1)
                    expert_out(2)
                    expert_hidden(4)
                if gnn:
                    for j in range(0, 2):
                        project(j)
                if moe:
                    expert_out(3)
                    expert_hidden(5)
                if gnn:
                    for j in range(2, 5):
                        project(j)
                if moe:
                    expert_out(4)
                    expert_hidden(6)
                if gnn:
                    for j in range(5, NJ):
                        project(j)
                if moe:
                    expert_out(5)
                    expert_hidden(7)
                if nxt:
                    aggregate()
                if moe:
                    expert_out(6)
                if gnn:
                    tokens_transposed()
                if moe:
                    expert_out(7)

            iterations(pe, body)


_INS = ['x', 'adj', 'L0_gnn_epsilon', 'L0_gnn_W1', 'L0_gnn_b1', 'L0_gnn_rms_weight', 'L0_gnn_W2', 'L0_gnn_b2',
        'L0_ffn_router_w', 'L0_ffn_w1', 'L0_ffn_b1', 'L0_ffn_w2', 'L0_ffn_b2']
_OUTS = [((128, 128, 256), 'float32')]


def kernel(**inputs):
    import numpy as _np
    import concourse.bacc as _bacc
    from concourse import mybir as _mybir
    from concourse.bass_utils import run_bass_kernel_spmd as _run

    nc = _bacc.Bacc("TRN2", target_bir_lowering=False, num_devices=1)
    arrays, args = {}, []
    for name in _INS:
        a = _np.ascontiguousarray(inputs[name])
        if a.ndim == 0:
            a = a.reshape(1)
        arrays[f"in_{name}_dram"] = a
        args.append(nc.dram_tensor(f"in_{name}_dram", a.shape, _mybir.dt.from_np(a.dtype), kind="ExternalInput").ap())
    for i, (shape, dtype) in enumerate(_OUTS):
        dt = _mybir.dt.from_np(_np.dtype(dtype))
        args.append(nc.dram_tensor(f"out_{i}_dram", shape, dt, kind="ExternalOutput").ap())
    gnn_moe_kernel(nc, *args)
    r = _run(nc, [arrays], core_ids=[0])
    got = tuple(r.results[0][f"out_{i}_dram"] for i in range(len(_OUTS)))
    return got[0]
```

```python
from contextlib import ExitStack

import concourse.bass as bass
from concourse import mybir


F32 = mybir.dt.float32
F32R = mybir.dt.float32r
U32 = mybir.dt.uint32
ALU = mybir.AluOpType
ACT = mybir.ActivationFunctionType
AX_X = mybir.AxisListType.X

P = 128
LN_EPS = 1e-5
RMS_EPS = 1e-6

def _events(NJ, NE, NT):
    ev = {}
    ev["bank"] = ([("logits", "moe")] + [(f"h{j}", "gnn") for j in range(NJ)]
                  + [("adjT", "next"), ("ss", "gnn"), ("rms", "gnn"),
                     ("combT", "moe"), ("b2_0", "moe"), ("b2_1", "moe"), ("agg0", "next"), ("agg1", "next"),
                     ("xT0", "gnn"), ("xT1", "gnn")])
    ev["hidden"] = [(f"{e}_{f}", "moe") for e in range(NE) for f in range(2)]
    ev["expert"] = [(f"{e}_{y}", "moe") for e in range(NE) for y in range(2)]
    ev["w2"] = [(f"{j}", "gnn") for j in range(NJ)]
    ev["gelu"] = [(f"{e}_{f}", "moe") for e in range(NE) for f in range(2)]
    ev["gelu_hi"] = [(f"{e}_{f}", "moe") for e in range(NE) for f in range(2)]
    ev["h_even"] = [(f"{j}", "gnn") for j in range(0, NJ, 2)]
    ev["sq"] = [(f"{j}", "gnn") for j in range(NJ)]
    ev["tanh"] = [(f"{j}", "gnn") for j in range(NJ)]
    ev["act_hi"] = [(f"{j}", "gnn") for j in range(NJ)]
    ev["hi"] = [("xn", "next"), ("adjT", "next"), ("agg0", "next"), ("agg1", "next"),
                ("xT0", "gnn"), ("xT1", "gnn")]
    ev["ln"] = ([(f"a_st{t}", "next") for t in range(NT)] + [(f"a_ag{t}", "next") for t in range(NT)]
                + [("a_var", "next")] + [(f"a_x{t}", "next") for t in range(NT)]
                + [(f"b_st{t}", "gnn") for t in range(NT)] + [(f"b_ag{t}", "gnn") for t in range(NT)]
                + [("b_var", "gnn")] + [(f"b_x{t}", "gnn") for t in range(NT)])
    ev["router"] = ([(n, "moe") for n in ["copy", "parts", "max", "shift", "sum", "rsum", "prob"]]
                    + [(f"top{t}", "moe") for t in range(NT)] + [(f"idx{t}", "moe") for t in range(NT)]
                    + [(n, "moe") for n in ["cast", "pair", "floor", "rpair", "w", "m0", "m1", "c0", "c1", "comb", "hi", "lo", "hi2", "combT"]])
    ev["lo"] = [("xn", "next"), ("adjT", "next"), ("agg0", "next"), ("agg1", "next"),
                ("xT0", "gnn"), ("xT1", "gnn")]
    ev["h_odd"] = [(f"{j}", "gnn") for j in range(1, NJ, 2)]
    ev["adj"] = [("epsI", "next")]
    ev["rms"] = [(n, "gnn") for n in ["ms", "hi", "lo", "diag_hi", "diag_lo"]]
    ev["y"] = [(f"{j}", "gnn") for j in range(NJ)]
    ev["silu"] = [(f"{j}", "gnn") for j in range(NJ)]
    ev["act_lo"] = [(f"{j}", "gnn") for j in range(NJ)]
    ev["x2"] = [("0", "gnn"), ("1", "gnn")]
    ev["b2"] = [("0", "moe"), ("1", "moe")]
    ev["acc"] = [(f"{e}_{y}", "moe") for e in range(NE) for y in range(2)]
    ev["pow"] = [("exp0", "moe"), ("a", "next"), ("exp1", "moe"), ("rms", "gnn"), ("b", "gnn")]
    ev["gelu_lo"] = [(f"{e}_{f}", "moe") for e in range(NE) for f in range(2)]
    ev["sumsq"] = [(f"{j}", "gnn") for j in range(1, NJ)]
    ev["xb"] = [("x", "next")]
    ev["acc0"] = [("xn2", "gnn")]
    return ev


def gnn_moe_kernel(nc, x, adj, eps, W1, b1, rms_w, W2, b2, router_w, w1, eb1, w2, eb2, out):
    NB, N, D = x.shape
    H = W1.shape[1]
    NE = router_w.shape[0]
    GB = 4
    T = GB * N
    NG = NB // GB
    NT = T // P
    KC = D // P
    NA = 3
    NJ = H // P
    assert (N, D, T, KC) == (P, 256, 512, 2)
    EV = _events(NJ, NE, NT)
    H_SEM = ["h_even", "h_odd"]

    def parts(i):
        return [n for n, on in (("next", -1 <= i < NG - 1), ("gnn", 0 <= i < NG), ("moe", 1 <= i <= NG)) if on]

    def count(sem, what, i):
        names = [n for n, _ in EV[sem]]
        where = names.index(what)
        part = EV[sem][where][1]
        if part not in parts(i):
            assert i < 2
            return 0
        total = 0
        for j in range(-1, i):
            total += sum(p in parts(j) for _, p in EV[sem])
        return total + sum(p in parts(i) for _, p in EV[sem][:where + 1])

    class Step:

        def __init__(self, n, k=None):
            self.n, self.k = n, k

        def back(self, d):
            return Step(self.n - d, self.k)

        def at(self, f):
            if self.k is None:
                return f(self.n)
            slope = f(self.n + 2) - f(self.n)
            assert f(self.n + 4) - f(self.n + 2) == slope
            return f(self.n) + self.k * slope

        def has(self, part):
            return part in parts(self.n)

    with ExitStack() as ctx:
        def sb(name, shape, dt=F32):
            return ctx.enter_context(nc.sbuf_tensor(name, shape, dt))

        W1_hi, W1_lo = sb("W1_hi", [P, KC, H], F32R), sb("W1_lo", [P, KC, H], F32R)
        W2_hi, W2_lo = sb("W2_hi", [P, NJ, D], F32R), sb("W2_lo", [P, NJ, D], F32R)
        w1_hi, w1_lo = sb("w1_hi", [P, NE, KC, D], F32R), sb("w1_lo", [P, NE, KC, D], F32R)
        w2_hi, w2_lo = sb("w2_hi", [P, NE, KC, D], F32R), sb("w2_lo", [P, NE, KC, D], F32R)
        wr_split = sb("wr_split", [P, KC, 2, NE], F32R)
        ident = sb("ident", [P, P])
        ones = sb("ones", [P, P], F32R)
        neg_half = sb("neg_half", [P, NT])
        e_base = sb("e_base", [P, NT, NE])
        expert_no = sb("expert_no", [P, NE])
        eps_col = sb("eps_col", [P, 1])
        ROWS = 2 * NJ + 2 * KC * NE
        cols = sb("cols", [P, ROWS])
        b1_col = cols[:, 0:NJ]
        rms_w_col = cols[:, NJ:2 * NJ]
        eb1_col = cols[:, 2 * NJ:2 * NJ + KC * NE].rearrange("p (e k) -> p e k", k=KC)
        wr = cols[:, 2 * NJ + KC * NE:ROWS].rearrange("p (k e) -> p k e", k=KC)
        half_w = sb("half_w", [P, NJ])
        b2_row = sb("b2_row", [P, D])
        eb2_stack = sb("eb2_stack", [3 * NE, D], F32R)
        low_row, high_row = sb("low_row", [3 * NE, 1]), sb("high_row", [3 * NE, 1])
        x_in = sb("x_in", [P, 2, GB, D])
        adj_in = sb("adj_in", [P, GB, N])
        acc = sb("acc", [P, 2, NT, D])
        xn = sb("xn", [P, NT, D])
        xn_hi, xn_lo = sb("xn_hi", [P, GB, D], F32R), sb("xn_lo", [P, GB, D], F32R)
        adjT_hi, adjT_lo = sb("adjT_hi", [P, GB, N], F32R), sb("adjT_lo", [P, GB, N], F32R)
        agg_hi, agg_lo = sb("agg_hi", [P, KC, T], F32R), sb("agg_lo", [P, KC, T], F32R)
        h = sb("h", [P, NJ, T])
        sq = sb("sq", [P, 2, T])
        sumsq = sb("sumsq", [P, T])
        ones_stage = sumsq[:, 0:P]
        tanh = sq
        rows = sq[0:ROWS, 0, 0:P]
        eb2_sb = sq[0:3 * NE, 1, 0:D]
        act_hi, act_lo = sb("act_hi", [P, NA, T], F32R), sb("act_lo", [P, NA, T], F32R)
        diag_hi, diag_lo = act_hi[:, 0, :], act_lo[:, 0, :]
        xT_hi, xT_lo = sb("xT_hi", [P, KC, T], F32R), sb("xT_lo", [P, KC, T], F32R)
        gelu = sb("gelu", [P, 2, T])
        gelu_hi, gelu_lo = sb("gelu_hi", [P, 2, KC, T], F32R), sb("gelu_lo", [P, 2, KC, T], F32R)
        stats = sb("stats", [P, 2, NT, 6])
        mean_var = sb("mean_var", [P, 2, NT, 2])
        var_eps = sb("var_eps", [P, 2, NT])
        rstd = sb("rstd", [P, 2, NT])
        ms_eps = sb("ms_eps", [P, NT])
        rrms = sb("rrms", [P, NT])
        rrms_hi, rrms_lo = sb("rrms_hi", [P, NT], F32R), sb("rrms_lo", [P, NT])
        logit2 = sb("logit2", [P, NT, 2, NE])
        logit = logit2[:, :, 0, :]
        top_logit = sb("top_logit", [P, NT])
        shifted = sb("shifted", [P, NT, NE])
        expd = sb("expd", [P, NT, NE])
        rsum = sb("rsum", [P, 2, NT])
        prob = expd
        top = sb("top", [P, NT, NE])
        top_at = sb("top_at", [P, NT, NE], U32)
        top_at_f = sb("top_at_f", [P, NT, 2])
        pair = sb("pair", [P, 3, NT])
        weight = sb("weight", [P, NT, 2])
        mask = sb("mask", [P, 2, NT, NE])
        comb = sb("comb", [P, NT, NE])
        comb_stack = sb("comb_stack", [P, NT, 3 * NE], F32R)
        combT = sb("combT", [3 * NE, T], F32R)

        def bank(name):
            return ctx.enter_context(nc.psum_tensor(name, [P, 512], F32))

        A = [bank("A0"), bank("A1")]
        O = [bank("O0"), bank("O1")]
        HB = [bank("H0"), bank("H1")]
        Y = [bank("Y0"), bank("Y1")]

        BANK_OF = {"logits": 0, **{f"h{j}": (j + 1) % 2 for j in range(NJ)}, "ss": 1, "combT": 0,
                   "adjT": 0, "rms": 1, "b2_0": 0, "b2_1": 0, "agg0": 0, "agg1": 1, "xT0": 0, "xT1": 1}

        S = {name: ctx.enter_context(nc.semaphore(f"s_{name}")) for name in EV}
        s_x = [ctx.enter_context(nc.semaphore(f"s_x{p}")) for p in range(2)]
        s_adj = ctx.enter_context(nc.semaphore("s_adj_in"))
        s_out = [ctx.enter_context(nc.semaphore(f"s_out{p}")) for p in range(2)]
        s_small = ctx.enter_context(nc.semaphore("s_small"))
        s_const = ctx.enter_context(nc.semaphore("s_const"))
        s_stage = [ctx.enter_context(nc.semaphore(f"s_stage{p}")) for p in range(2 + NE)]
        s_whi = ctx.enter_context(nc.semaphore("s_whi"))
        s_wlo = ctx.enter_context(nc.semaphore("s_wlo"))
        s_passed = ctx.enter_context(nc.semaphore("s_passed"))
        s_wr = ctx.enter_context(nc.semaphore("s_wr"))
        s_turned = ctx.enter_context(nc.semaphore("s_turned"))
        s_cols = ctx.enter_context(nc.semaphore("s_cols"))
        s_ones = ctx.enter_context(nc.semaphore("s_ones"))
        s_eb2 = ctx.enter_context(nc.semaphore("s_eb2"))
        s_halfw = ctx.enter_context(nc.semaphore("s_halfw"))

        def wait(eng, sem, what, it):
            v = it.at(lambda i: count(sem, what, i))
            if it.k is None and v <= 0:
                return
            assert it.k is not None or v > 0
            assert count(sem, what, it.n) > 0, (sem, what, it.n)
            eng.wait_ge(S[sem], v)

        def wait_alone(eng, sem, what, it):
            wait(eng, sem, what, it)
            eng.sem_inc(s_passed, 1)

        def loaded(eng, sem, it, g, per=2):
            eng.wait_ge(sem, it.at(lambda i: 16 * (g(i) // per + 1)))

        SMALL = 16 * 10
        CONST = 8

        def iterations(eng, body, first=-1):
            for i in range(first, 2):
                body(Step(i))
            with eng.Fori(0, (NG - 4) // 2) as k:
                body(Step(2, k))
                body(Step(3, k))
            for i in range(NG - 2, NG + 1):
                body(Step(i))

        gelu_stage = gelu[:, :, :].rearrange("p f t -> p (f t)")
        acc_stage = acc[:, 1, :, :].rearrange("p t d -> p (t d)")
        STAGES = [
            (h[:, 0:NJ // 2, :].rearrange("p j t -> p (j t)"), W1.rearrange("(k p) h -> p k h", p=P),
             W1_hi[:, :, :].rearrange("p k h -> p (k h)"), W1_lo[:, :, :].rearrange("p k h -> p (k h)")),
            (h[:, NJ // 2:NJ, :].rearrange("p j t -> p (j t)"), W2.rearrange("(j p) d -> p j d", p=P),
             W2_hi[:, :, :].rearrange("p j d -> p (j d)"), W2_lo[:, :, :].rearrange("p j d -> p (j d)")),
        ]
        for w, hi, lo in ((w1, w1_hi, w1_lo), (w2, w2_hi, w2_lo)):
            for e in range(0, NE, 2):
                STAGES.append(([gelu_stage, acc_stage][(e // 2) % 2],
                               w[e:e + 2].rearrange("e (k p) f -> p (e k) f", p=P),
                               hi[:, e:e + 2, :, :].rearrange("p e k f -> p (e k f)"),
                               lo[:, e:e + 2, :, :].rearrange("p e k f -> p (e k f)")))
        STAGES_AT = {2: (4, 5), 4: (6, 7), 6: (8, 9)}

        def split_high(act, n):
            src, _, hi, _ = STAGES[n]
            act.wait_ge(s_stage[n], 16)
            act.activation(hi, src, ACT.Copy).then_inc(s_whi, 1)

        def split_low(dve, n):
            src, _, hi, lo = STAGES[n]
            dve.wait_ge(s_whi, n + 1)
            dve.tensor_tensor(lo, src, hi.bitcast(F32), ALU.subtract).then_inc(s_wlo, 1)

        block = ctx.enter_context(nc.Block())

        @block.sync
        def _(sp):
            def load_x(it, g, p):
                sp.dma_start(x_in[:, p, :, :], x[bass.ds(g * GB, GB), :, :].rearrange("b n d -> n b d")).then_inc(s_x[p], 16)

            def load_adj(it, g):
                sp.dma_start(adj_in[:, :, :], adj[bass.ds(g * GB, GB), :, :].rearrange("b n m -> n b m")).then_inc(s_adj, 16)

            def store(it, g, p):
                wait(sp, "acc", f"{NE - 1}_1", it)
                sp.dma_start(out[bass.ds(g * GB, GB), :, :].rearrange("b n d -> n b d"), acc[:, p, :, :]).then_inc(s_out[p], 16)

            def stage(n):
                dst, src, _, _ = STAGES[n]
                if n >= 4:
                    sp.wait_ge(s_wlo, n - 1)
                sp.dma_start(dst.rearrange("p (a b) -> p a b", b=src.shape[2]), src).then_inc(s_stage[n], 16)

            load_x(None, 0, 0)
            load_adj(None, 0)
            stage(0)
            load_x(None, 1, 1)
            stage(1)
            stage(2)
            stage(3)
            wait(sp, "lo", "adjT", Step(-1))
            load_adj(None, 1)
            for n in range(4, len(STAGES)):
                stage(n)

            def body(it, g, p):
                wait(sp, "lo", "adjT", it)
                load_adj(it, g)
                wait(sp, "x2", "1", it)
                load_x(it, g, p)
                if it.has("moe"):
                    store(it, g - 3, 1 - p)

            body(Step(0), 2, 0)
            body(Step(1), 3, 1)
            with sp.Fori(0, (NG - 4) // 2) as k:
                body(Step(2, k), k * 2 + 4, 0)
                body(Step(3, k), k * 2 + 5, 1)
            for i in range(NG - 2, NG + 1):
                store(Step(i), i - 1, (i - 1) % 2)
            sp.wait_ge(s_out[0], 16 * (NG // 2))
            sp.wait_ge(s_out[1], 16 * (NG // 2))

        @block.gpsimd
        def _(pool):
            pool.memset(ident[:, :], 0.0).then_inc(s_const, 1)
            pool.memset(ones_stage, 1.0).then_inc(s_const, 1)
            pool.memset(neg_half[:, :], -0.5).then_inc(s_const, 1)
            pool.memset(e_base[:, :, :], 2.718281828459045).then_inc(s_const, 1)
            pool.iota(expert_no[:, :], [[1, NE]], base=0, channel_multiplier=0,
                      allow_small_or_imprecise_dtypes=True).then_inc(s_const, 1)
            pool.memset(low_row[:, :], 1.0).then_inc(s_const, 1)
            pool.wait_ge(s_const, 6)
            pool.affine_select(out=low_row[:, :], in_=low_row[:, :], compare_op=ALU.is_ge, fill=0.0, base=-2 * NE,
                               pattern=[[0, 1]], channel_multiplier=1).then_inc(s_const, 1)
            pool.affine_select(out=ident[:, :], in_=ident[:, :], compare_op=ALU.not_equal, fill=1.0, base=0,
                               pattern=[[-1, P]], channel_multiplier=1).then_inc(s_const, 1)
            pool.wait_ge(s_const, CONST)
            pool.wait_ge(s_small, SMALL)

            def body(it):
                prev = it.back(1)
                moe, gnn, nxt = it.has("moe"), it.has("gnn"), it.has("next")
                p = it.n % 2

                def gelu_low(e):
                    for f in range(2):
                        wait(pool, "gelu_hi", f"{e}_{f}", it)
                        if e >= 2:
                            wait(pool, "expert", f"{e - 2}_1", it)
                        elif prev.has("moe"):
                            wait(pool, "expert", f"{NE + e - 2}_1", prev)
                        pool.tensor_tensor(gelu_lo[:, e % 2, f, :], gelu[:, f, :], gelu_hi[:, e % 2, f, :].bitcast(F32),
                                           ALU.subtract).then_inc(S["gelu_lo"], 1)

                def add_square(j):
                    wait(pool, "sq", f"{j}", it)
                    if j == 1:
                        if prev.has("gnn"):
                            wait(pool, "bank", "rms", prev)
                        else:
                            pool.wait_ge(s_ones, 1)
                        pool.tensor_tensor(sumsq[:, :], sq[:, 0, :], sq[:, 1, :], ALU.add).then_inc(S["sumsq"], 1)
                    elif j > 1:
                        wait(pool, "sumsq", f"{j - 1}", it)
                        pool.tensor_tensor(sumsq[:, :], sumsq[:, :], sq[:, j % 2, :], ALU.add).then_inc(S["sumsq"], 1)

                def exponentials(half):
                    if half == 0:
                        wait(pool, "router", "shift", it)
                    ts = slice(2 * half, 2 * half + 2)
                    pool.tensor_tensor(expd[:, ts, :], e_base[:, ts, :], shifted[:, ts, :], ALU.pow).then_inc(S["pow"], 1)

                if moe:
                    exponentials(0)
                if nxt:
                    wait(pool, "ln", "a_var", it)
                    pool.tensor_tensor(rstd[:, 0, :], var_eps[:, 0, :], neg_half[:, :], ALU.pow).then_inc(S["pow"], 1)
                if moe:
                    gelu_low(0)
                    exponentials(1)
                if gnn:
                    add_square(1)
                if moe:
                    gelu_low(1)
                if gnn:
                    for j in range(2, NJ):
                        add_square(j)
                if moe:
                    gelu_low(2)
                if gnn:
                    wait(pool, "rms", "ms", it)
                    pool.tensor_tensor(rrms[:, :], ms_eps[:, :], neg_half[:, :], ALU.pow).then_inc(S["pow"], 1)
                if moe:
                    for e in range(3, 6):
                        gelu_low(e)
                if nxt:
                    wait(pool, "ln", f"a_x{NT - 1}", it)
                    pool.tensor_tensor(x_in[:, 1 - p, :, :], x_in[:, 1 - p, :, :],
                                       b2_row[:, :].unsqueeze(1).broadcast_to([P, GB, D]), ALU.add).then_inc(S["xb"], 1)
                if moe:
                    gelu_low(6)
                if gnn:
                    wait(pool, "ln", "b_var", it)
                    pool.tensor_tensor(rstd[:, 1, :], var_eps[:, 1, :], neg_half[:, :], ALU.pow).then_inc(S["pow"], 1)
                if moe:
                    gelu_low(7)
                if gnn:
                    wait(pool, "ln", f"b_x{NT - 1}", it)
                    pool.tensor_tensor(acc[:, p, :, :], acc[:, p, :, :], xn[:, :, :], ALU.add).then_inc(S["acc0"], 1)

            iterations(pool, body)

        @block.scalar
        def _(act):
            act.dma_start(rows[0:NJ], b1.rearrange("(j p) -> j p", p=P)).then_inc(s_small, 16)
            act.dma_start(rows[NJ:2 * NJ], rms_w.rearrange("(j p) -> j p", p=P)).then_inc(s_small, 16)
            r0 = 2 * NJ
            act.dma_start(rows[r0:r0 + KC * NE], eb1.rearrange("e (k p) -> (e k) p", p=P)).then_inc(s_small, 16)
            for kc in range(KC):
                r0 = 2 * NJ + KC * NE + kc * NE
                act.dma_start(rows[r0:r0 + NE], router_w[:, kc * P:(kc + 1) * P]).then_inc(s_small, 16)
            for s in range(3):
                act.dma_start(sq[s * NE:(s + 1) * NE, 1, 0:D], eb2).then_inc(s_small, 16)
            act.dma_start(eps_col[:, :], eps.partition_broadcast(P)).then_inc(s_small, 16)
            act.dma_start(b2_row[:, :], b2.partition_broadcast(P)).then_inc(s_small, 16)
            act.wait_ge(s_small, SMALL)
            act.wait_ge(s_cols, 1)

            def body(it):
                prev = it.back(1)
                moe, gnn, nxt = it.has("moe"), it.has("gnn"), it.has("next")

                def gelus(e):
                    for f in range(2):
                        wait(act, "hidden", f"{e}_{f}", it)
                        if e >= 1:
                            wait(act, "gelu_lo", f"{e - 1}_{f}", it)
                        elif prev.has("moe"):
                            wait(act, "gelu_lo", f"{NE - 1}_{f}", prev)
                        act.activation(gelu[:, f, :], HB[f][:, :], ACT.Gelu,
                                       bias=eb1_col[:, e, f:f + 1]).then_inc(S["gelu"], 1)

                def gelu_high(e):
                    for f in range(2):
                        wait(act, "gelu", f"{e}_{f}", it)
                        if e >= 2:
                            wait(act, "expert", f"{e - 2}_1", it)
                        elif prev.has("moe"):
                            wait(act, "expert", f"{NE + e - 2}_1", prev)
                        act.activation(gelu_hi[:, e % 2, f, :], gelu[:, f, :], ACT.Copy).then_inc(S["gelu_hi"], 1)

                def hidden_rows(j):
                    wait(act, "bank", f"h{j}", it)
                    if prev.has("gnn"):
                        wait(act, "act_lo", f"{j}", prev)
                    elif it.n == 0:
                        act.wait_ge(s_wlo, 2)
                    act.activation(h[:, j, :], A[BANK_OF[f"h{j}"]][:, :], ACT.Identity,
                                   bias=b1_col[:, j:j + 1]).then_inc(S["h_even"], 1)

                def squares(a, b):
                    for j in range(a, b):
                        wait(act, H_SEM[j % 2], f"{j}", it)
                        if j == 2:
                            wait(act, "sumsq", "1", it)
                        elif j > 2:
                            wait(act, "sumsq", f"{j - 2}", it)
                        elif prev.has("gnn"):
                            wait(act, "silu", f"{NJ - 2 + j}", prev)
                        act.activation(sq[:, j % 2, :], h[:, j, :], ACT.Square).then_inc(S["sq"], 1)

                def tanhs(a, b):
                    for j in range(a, b):
                        wait(act, "y", f"{j}", it)
                        if j >= 2:
                            wait(act, "silu", f"{j - 2}", it)
                        else:
                            wait(act, "sumsq", f"{NJ - 1}", it)
                        act.activation(tanh[:, j % 2, :], h[:, j, :], ACT.Tanh).then_inc(S["tanh"], 1)

                def silu_high(a, b):
                    for j in range(a, b):
                        wait(act, "silu", f"{j}", it)
                        if j >= NA:
                            wait(act, "w2", f"{j - NA}", it)
                        elif prev.has("gnn"):
                            wait(act, "w2", f"{NJ - 1}", prev)
                        act.activation(act_hi[:, j % NA, :], h[:, j, :], ACT.Copy).then_inc(S["act_hi"], 1)

                def stages(slot):
                    if it.n == 0:
                        for n in STAGES_AT[slot]:
                            split_high(act, n)

                if moe:
                    gelus(0)
                if gnn:
                    hidden_rows(0)
                if moe:
                    gelu_high(0)
                if gnn:
                    hidden_rows(2)
                    squares(0, 2)
                if moe:
                    gelus(1)
                if gnn:
                    hidden_rows(4)
                    squares(2, 3)
                if moe:
                    gelu_high(1)
                if gnn:
                    hidden_rows(6)
                    squares(3, 4)
                if nxt:
                    wait(act, "ln", f"a_x{NT - 1}", it)
                    if prev.has("next"):
                        wait(act, "bank", "agg1", prev)
                    act.activation(xn_hi[:, :, :], xn[:, :, :], ACT.Copy).then_inc(S["hi"], 1)
                if gnn:
                    squares(4, 7)
                if moe:
                    gelus(2)
                if gnn:
                    squares(7, 8)
                if moe:
                    gelu_high(2)
                if nxt:
                    wait(act, "adj", "epsI", it)
                    act.activation(adjT_hi[:, :, :], adj_in[:, :, :], ACT.Copy).then_inc(S["hi"], 1)
                stages(2)
                if moe:
                    gelus(3)
                    gelu_high(3)
                if gnn:
                    tanhs(0, 2)
                    silu_high(0, 2)
                if moe:
                    gelus(4)
                if gnn:
                    tanhs(2, 4)
                    silu_high(2, 3)
                if moe:
                    gelu_high(4)
                if gnn:
                    tanhs(4, 6)
                    silu_high(3, 5)
                stages(4)
                if moe:
                    gelus(5)
                if gnn:
                    tanhs(6, 8)
                if moe:
                    gelu_high(5)
                if gnn:
                    silu_high(5, 8)
                if moe:
                    gelus(6)
                    gelu_high(6)
                stages(6)
                if moe:
                    gelus(7)
                if nxt:
                    for c in range(KC):
                        wait(act, "bank", f"agg{c}", it)
                        act.activation(agg_hi[:, c, :], A[BANK_OF[f"agg{c}"]][:, :], ACT.Copy).then_inc(S["hi"], 1)
                if moe:
                    gelu_high(7)
                if gnn:
                    for c in range(KC):
                        wait(act, "bank", f"xT{c}", it)
                        act.activation(xT_hi[:, c, :], A[BANK_OF[f"xT{c}"]][:, :], ACT.Copy).then_inc(S["hi"], 1)

            split_high(act, 0)
            body(Step(-1))
            for n in range(1, 4):
                split_high(act, n)
            iterations(act, body, 0)

        @block.vector
        def _(dve):
            dve.wait_ge(s_const, CONST)
            dve.wait_ge(s_small, SMALL)
            dve.tensor_copy(ones[:, :], ones_stage).then_inc(s_ones, 1)
            dve.wait_ge(s_turned, 1)
            dve.tensor_copy(cols[:, :], A[1][:, 0:ROWS]).then_inc(s_cols, 1)
            dve.wait_ge(s_cols, 1)
            dve.tensor_copy(wr_split[:, :, 0, :], wr).then_inc(s_wr, 1)
            dve.wait_ge(s_wr, 1)
            dve.tensor_tensor(wr_split[:, :, 1, :], wr, wr_split[:, :, 0, :].bitcast(F32), ALU.subtract).then_inc(s_wr, 1)
            dve.tensor_copy(eb2_stack[:, :], eb2_sb).then_inc(s_eb2, 1)
            dve.wait_ge(s_eb2, 1)
            dve.tensor_tensor(eb2_sb, eb2_sb, eb2_stack[:, :].bitcast(F32), ALU.subtract).then_inc(s_eb2, 1)
            dve.wait_ge(s_eb2, 2)
            dve.tensor_scalar(eb2_sb, eb2_sb, low_row[:, 0:1], None, ALU.mult).then_inc(s_eb2, 1)
            dve.tensor_scalar(high_row[:, :], low_row[:, :], 1.0, -1.0, ALU.subtract, ALU.mult).then_inc(s_eb2, 1)
            dve.wait_ge(s_eb2, 4)
            dve.scalar_tensor_tensor(out=eb2_stack[:, :], in0=eb2_stack[:, :].bitcast(F32), scalar=high_row[:, 0:1],
                                     in1=eb2_sb, op0=ALU.mult, op1=ALU.add).then_inc(s_eb2, 1)
            dve.tensor_scalar(half_w[:, :], rms_w_col, 0.5, None, ALU.mult).then_inc(s_halfw, 1)
            dve.wait_ge(s_halfw, 1)

            def body(it):
                prev = it.back(1)
                moe, gnn, nxt = it.has("moe"), it.has("gnn"), it.has("next")
                p = it.n % 2
                q = 1 - p

                def norm_stats(which, part, src):
                    for t in range(NT):
                        dve.bn_stats(stats[:, part, t, :], src[:, t, :]).then_inc(S["ln"], 1)
                    wait_alone(dve, "ln", f"{which}_st{NT - 1}", it)
                    for t in range(NT):
                        dve.bn_aggr(mean_var[:, part, t, :], stats[:, part, t, :]).then_inc(S["ln"], 1)
                    wait(dve, "ln", f"{which}_ag{NT - 1}", it)
                    dve.tensor_scalar(var_eps[:, part, :], mean_var[:, part, :, 1], LN_EPS, None,
                                      ALU.add).then_inc(S["ln"], 1)

                def norm_apply(which, part, src):
                    wait(dve, "pow", which, it)
                    for t in range(NT):
                        dve.tensor_scalar(xn[:, t, :], src[:, t, :], mean_var[:, part, t, 0:1], rstd[:, part, t:t + 1],
                                          ALU.subtract, ALU.mult).then_inc(S["ln"], 1)

                def router_shift():
                    wait(dve, "bank", "logits", it)
                    dve.tensor_copy(logit2[:, :, :, :], A[0][:, 0:2 * NT * NE].rearrange("p (t s e) -> p t s e", t=NT, s=2)).then_inc(S["router"], 1)
                    wait(dve, "router", "copy", it)
                    dve.tensor_tensor(logit, logit2[:, :, 0, :], logit2[:, :, 1, :], ALU.add).then_inc(S["router"], 1)
                    wait(dve, "router", "parts", it)
                    dve.tensor_reduce(top_logit[:, :], logit, AX_X, ALU.max).then_inc(S["router"], 1)
                    wait(dve, "router", "max", it)
                    if prev.has("moe"):
                        wait(dve, "pow", "exp1", prev)
                    dve.tensor_tensor(shifted[:, :, :], logit, top_logit[:, :].unsqueeze(2).broadcast_to([P, NT, NE]),
                                      ALU.subtract).then_inc(S["router"], 1)

                def router_top():
                    wait(dve, "pow", "exp1", it)
                    dve.tensor_reduce(rsum[:, 0, :], expd[:, :, :], AX_X, ALU.add).then_inc(S["router"], 1)
                    wait(dve, "router", "sum", it)
                    dve.reciprocal(rsum[:, 1, :], rsum[:, 0, :]).then_inc(S["router"], 1)
                    wait(dve, "router", "rsum", it)
                    dve.tensor_tensor(prob[:, :, :], expd[:, :, :], rsum[:, 1, :].unsqueeze(2).broadcast_to([P, NT, NE]),
                                      ALU.mult).then_inc(S["router"], 1)
                    wait_alone(dve, "router", "prob", it)
                    for t in range(NT):
                        dve.max(top[:, t, :], prob[:, t, :]).then_inc(S["router"], 1)
                    wait_alone(dve, "router", f"top{NT - 1}", it)
                    for t in range(NT):
                        dve.max_index(top_at[:, t, :], top[:, t, :], prob[:, t, :]).then_inc(S["router"], 1)
                    wait(dve, "router", f"idx{NT - 1}", it)
                    dve.tensor_copy(top_at_f[:, :, :], top_at[:, :, 0:2]).then_inc(S["router"], 1)

                def router_combine():
                    dve.tensor_tensor(pair[:, 0, :], top[:, :, 0], top[:, :, 1], ALU.add).then_inc(S["router"], 1)
                    wait(dve, "router", "pair", it)
                    dve.tensor_scalar(pair[:, 1, :], pair[:, 0, :], 1e-12, None, ALU.max).then_inc(S["router"], 1)
                    wait(dve, "router", "floor", it)
                    dve.reciprocal(pair[:, 2, :], pair[:, 1, :]).then_inc(S["router"], 1)
                    wait(dve, "router", "rpair", it)
                    dve.tensor_tensor(weight[:, :, :], top[:, :, 0:2], pair[:, 2, :].unsqueeze(2).broadcast_to([P, NT, 2]),
                                      ALU.mult).then_inc(S["router"], 1)
                    for m in range(2):
                        dve.tensor_tensor(mask[:, m, :, :], expert_no[:, :].unsqueeze(1).broadcast_to([P, NT, NE]),
                                          top_at_f[:, :, m:m + 1].broadcast_to([P, NT, NE]), ALU.is_equal).then_inc(S["router"], 1)
                    for m in range(2):
                        wait(dve, "router", f"m{m}", it)
                        dve.tensor_tensor(mask[:, m, :, :], mask[:, m, :, :], weight[:, :, m:m + 1].broadcast_to([P, NT, NE]),
                                          ALU.mult).then_inc(S["router"], 1)
                    wait(dve, "router", "c1", it)
                    if prev.has("moe"):
                        wait(dve, "bank", "combT", prev)
                        wait(dve, "acc", f"{NE - 1}_1", prev)
                    dve.tensor_tensor(comb[:, :, :], mask[:, 0, :, :], mask[:, 1, :, :], ALU.add).then_inc(S["router"], 1)
                    wait(dve, "router", "comb", it)
                    dve.tensor_copy(comb_stack[:, :, 0:NE], comb[:, :, :]).then_inc(S["router"], 1)
                    wait(dve, "router", "hi", it)
                    dve.tensor_tensor(comb_stack[:, :, NE:2 * NE], comb[:, :, :], comb_stack[:, :, 0:NE].bitcast(F32),
                                      ALU.subtract).then_inc(S["router"], 1)
                    dve.tensor_copy(comb_stack[:, :, 2 * NE:3 * NE], comb_stack[:, :, 0:NE].bitcast(F32)).then_inc(S["router"], 1)

                def expert_sum(e):
                    if e == 0:
                        wait(dve, "router", "comb", it)
                        wait(dve, "acc0", "xn2", prev)
                    else:
                        wait(dve, "acc", f"{e - 1}_1", it)
                    if e in (4, 5):
                        wait(dve, "b2", f"{e - 4}", it)
                    for y in range(2):
                        wait(dve, "expert", f"{e}_{y}", it)
                        for t in range(2):
                            tt = 2 * y + t
                            last = dve.scalar_tensor_tensor(out=acc[:, q, tt, :], in0=Y[y][:, t * D:(t + 1) * D],
                                                            scalar=comb[:, tt, e:e + 1], in1=acc[:, q, tt, :],
                                                            op0=ALU.mult, op1=ALU.add)
                        last.then_inc(S["acc"], 1)

                def y_row(j):
                    if j == 0:
                        wait(dve, "bank", "rms", it)
                    wait(dve, H_SEM[j % 2], f"{j}", it)
                    dve.scalar_tensor_tensor(out=h[:, j, :], in0=h[:, j, :], scalar=half_w[:, j:j + 1], in1=A[1][:, :],
                                             op0=ALU.mult, op1=ALU.mult).then_inc(S["y"], 1)

                def silu_rows(a, b):
                    for j in range(a, b):
                        wait(dve, "tanh", f"{j}", it)
                        dve.scalar_tensor_tensor(out=h[:, j, :], in0=tanh[:, j % 2, :], scalar=1.0, in1=h[:, j, :],
                                                 op0=ALU.add, op1=ALU.mult).then_inc(S["silu"], 1)

                def silu_low(a, b):
                    for j in range(a, b):
                        wait(dve, "act_hi", f"{j}", it)
                        dve.tensor_tensor(act_lo[:, j % NA, :], h[:, j, :], act_hi[:, j % NA, :].bitcast(F32),
                                          ALU.subtract).then_inc(S["act_lo"], 1)

                def add_b2(y):
                    wait(dve, "bank", f"b2_{y}", it)
                    wait(dve, "acc", f"{3 + y}_1", it)
                    a = acc[:, q, 2 * y:2 * y + 2, :].rearrange("p t d -> p (t d)")
                    dve.tensor_tensor(a, A[BANK_OF[f"b2_{y}"]][:, :], a, ALU.add).then_inc(S["b2"], 1)

                def low_of_bank(name, lo, hi):
                    wait(dve, "hi", name, it)
                    dve.tensor_tensor(lo, A[BANK_OF[name]][:, :], hi.bitcast(F32), ALU.subtract).then_inc(S["lo"], 1)

                def hidden_rows(j):
                    wait(dve, "bank", f"h{j}", it)
                    if prev.has("gnn"):
                        wait(dve, "act_lo", f"{j}", prev)
                    elif it.n == 0:
                        dve.wait_ge(s_wlo, 2)
                    dve.tensor_scalar(h[:, j, :], A[BANK_OF[f"h{j}"]][:, :], b1_col[:, j:j + 1], None,
                                      ALU.add).then_inc(S["h_odd"], 1)

                def stages(slot):
                    if it.n == 0:
                        for n in STAGES_AT[slot]:
                            split_low(dve, n)

                if moe:
                    router_shift()
                if nxt:
                    loaded(dve, s_x[q], it, lambda i: i + 1)
                    norm_stats("a", 0, x_in[:, q])
                if gnn:
                    hidden_rows(1)
                if nxt:
                    if prev.has("gnn"):
                        wait(dve, "acc0", "xn2", prev)
                    norm_apply("a", 0, x_in[:, q])
                if gnn:
                    hidden_rows(3)
                if moe:
                    router_top()
                if gnn:
                    hidden_rows(5)
                if moe:
                    router_combine()
                if gnn:
                    hidden_rows(7)
                if moe:
                    expert_sum(0)
                if nxt:
                    wait(dve, "hi", "xn", it)
                    dve.tensor_tensor(xn_lo[:, :, :], xn[:, :, :], xn_hi[:, :, :].bitcast(F32), ALU.subtract).then_inc(S["lo"], 1)
                if nxt:
                    wait(dve, "bank", "adjT", it)
                    dve.scalar_tensor_tensor(out=adj_in[:, :, :], in0=ident[:, :].unsqueeze(1).broadcast_to([P, GB, N]),
                                             scalar=eps_col[:, 0:1], in1=A[0][:, :].rearrange("p (b n) -> p b n", b=GB),
                                             op0=ALU.mult, op1=ALU.add).then_inc(S["adj"], 1)
                if moe:
                    expert_sum(1)
                if nxt:
                    wait(dve, "hi", "adjT", it)
                    dve.tensor_tensor(adjT_lo[:, :, :], adj_in[:, :, :], adjT_hi[:, :, :].bitcast(F32), ALU.subtract).then_inc(S["lo"], 1)
                if gnn:
                    wait(dve, "bank", "ss", it)
                    dve.tensor_scalar(ms_eps[:, :], A[1][:, 0:NT], 1.0 / H, RMS_EPS, ALU.mult, ALU.add).then_inc(S["rms"], 1)
                if gnn:
                    wait(dve, "pow", "rms", it)
                    dve.tensor_copy(rrms_hi[:, :], rrms[:, :]).then_inc(S["rms"], 1)
                    wait(dve, "rms", "hi", it)
                    dve.tensor_tensor(rrms_lo[:, :], rrms[:, :], rrms_hi[:, :].bitcast(F32), ALU.subtract).then_inc(S["rms"], 1)
                    for diag, part, dep in ((diag_hi, rrms_hi[:, :].bitcast(F32), "hi"), (diag_lo, rrms_lo[:, :], "lo")):
                        wait(dve, "rms", dep, it)
                        dve.tensor_tensor(diag.rearrange("p (t n) -> p t n", t=NT), ident[:, :].unsqueeze(1).broadcast_to([P, NT, P]),
                                          part.unsqueeze(2).broadcast_to([P, NT, P]), ALU.mult).then_inc(S["rms"], 1)
                stages(2)
                if moe:
                    expert_sum(2)
                if gnn:
                    y_row(0)
                    y_row(1)
                    silu_rows(0, 2)
                    y_row(2)
                    y_row(3)
                    silu_low(0, 2)
                if gnn:
                    silu_rows(2, 3)
                    y_row(4)
                    y_row(5)
                    silu_rows(3, 4)
                    silu_low(2, 3)
                    y_row(6)
                    y_row(7)
                if moe:
                    wait(dve, "bank", "combT", it)
                    dve.tensor_copy(combT[:, :], A[0][0:3 * NE, :]).then_inc(S["router"], 1)
                if gnn:
                    silu_rows(4, 5)
                    silu_low(3, 4)
                stages(4)
                if moe:
                    expert_sum(3)
                if gnn:
                    silu_rows(5, 6)
                    silu_low(4, 5)
                    silu_rows(6, 8)
                    silu_low(5, 7)
                if moe:
                    add_b2(0)
                    expert_sum(4)
                if gnn:
                    silu_low(7, 8)
                stages(6)
                if moe:
                    add_b2(1)
                    expert_sum(5)
                if gnn:
                    wait(dve, "w2", f"{NJ - 1}", it)
                    wait(dve, "xb", "x", prev)
                    if it.n >= 2:
                        dve.wait_ge(s_out[p], it.at(lambda i: 16 * (i // 2)))
                    for y in range(2):
                        dve.tensor_tensor(acc[:, p, 2 * y:2 * y + 2, :].rearrange("p t d -> p (t d)"), O[y][:, :],
                                          x_in[:, p, 2 * y:2 * y + 2, :].rearrange("p t d -> p (t d)"),
                                          ALU.add).then_inc(S["x2"], 1)
                    wait(dve, "x2", "1", it)
                    norm_stats("b", 1, acc[:, p])
                if nxt:
                    for c in range(KC):
                        low_of_bank(f"agg{c}", agg_lo[:, c, :], agg_hi[:, c, :])
                if gnn:
                    norm_apply("b", 1, acc[:, p])
                if moe:
                    expert_sum(6)
                if gnn:
                    for c in range(KC):
                        low_of_bank(f"xT{c}", xT_lo[:, c, :], xT_hi[:, c, :])
                if moe:
                    expert_sum(7)

            split_low(dve, 0)
            body(Step(-1))
            for n in range(1, 4):
                split_low(dve, n)
            iterations(dve, body, 0)

        @block.tensor
        def _(pe):
            pe.wait_ge(s_const, CONST)
            pe.wait_ge(s_small, SMALL)
            pe.transpose(A[1][:, 0:ROWS], rows, ident[0:ROWS, 0:ROWS]).then_inc(s_turned, 1)

            def three(dst, hi, lo, m_hi, m_lo, start, stop):
                pe.matmul(dst, hi, m_hi, start=start, stop=False, skip_group_check=True)
                pe.matmul(dst, hi, m_lo, start=False, stop=False, skip_group_check=True)
                return pe.matmul(dst, lo, m_hi, start=False, stop=stop, skip_group_check=True)

            def body(it):
                prev = it.back(1)
                moe, gnn, nxt = it.has("moe"), it.has("gnn"), it.has("next")

                def expert_hidden(e, fs=(0, 1)):
                    for f in fs:
                        if e >= 1:
                            wait(pe, "gelu", f"{e - 1}_{f}", it)
                        elif prev.has("moe"):
                            wait(pe, "gelu", f"{NE - 1}_{f}", prev)
                        if e == 0 and f == 0:
                            wait(pe, "lo", "xT1", prev)
                        for c in range(KC):
                            cols_f = slice(f * P, (f + 1) * P)
                            mm = three(HB[f][:, :], w1_hi[:, e, c, cols_f], w1_lo[:, e, c, cols_f], xT_hi[:, c, :], xT_lo[:, c, :],
                                       c == 0, c == KC - 1)
                        mm.then_inc(S["hidden"], 1)

                def expert_out(e):
                    for f in range(2):
                        wait(pe, "gelu_lo", f"{e}_{f}", it)
                    for y in range(2):
                        if e >= 1:
                            wait(pe, "acc", f"{e - 1}_{y}", it)
                        elif prev.has("moe"):
                            wait(pe, "acc", f"{NE - 1}_{y}", prev)
                        for t in range(2):
                            ts = slice((2 * y + t) * P, (2 * y + t + 1) * P)
                            for f in range(2):
                                mm = three(Y[y][:, t * D:(t + 1) * D], gelu_hi[:, e % 2, f, ts], gelu_lo[:, e % 2, f, ts],
                                           w2_hi[:, e, f, :], w2_lo[:, e, f, :], f == 0, f == 1)
                        mm.then_inc(S["expert"], 1)

                def hidden_rows(j):
                    if j == 0:
                        wait(pe, "lo", "xT1", prev)
                        wait(pe, "lo", "agg1", prev)
                        if it.n == 0:
                            pe.wait_ge(s_wlo, 1)
                    elif j == 1:
                        if moe:
                            wait(pe, "router", "copy", it)
                        else:
                            wait(pe, "lo", "agg0", prev)
                    else:
                        wait(pe, H_SEM[j % 2], f"{j - 2}", it)
                    js = slice(j * P, (j + 1) * P)
                    for c in range(KC):
                        mm = three(A[BANK_OF[f"h{j}"]][:, :], W1_hi[:, c, js], W1_lo[:, c, js], agg_hi[:, c, :], agg_lo[:, c, :],
                                   c == 0, c == KC - 1)
                    mm.then_inc(S["bank"], 1)

                def logits():
                    wait(pe, "lo", "xT1", prev)
                    if nxt or prev.has("next"):
                        wait(pe, "lo", "agg1", prev)
                    if it.n == 1:
                        pe.wait_ge(s_wr, 2)
                    for t in range(NT):
                        both = A[0][:, 2 * t * NE:2 * (t + 1) * NE]
                        ts = slice(t * P, (t + 1) * P)
                        for c in range(KC):
                            w_both = wr_split[:, c, :, :].rearrange("p s e -> p (s e)")
                            pe.matmul(both, xT_hi[:, c, ts], w_both, start=c == 0, stop=False, skip_group_check=True)
                        for c in range(KC):
                            mm = pe.matmul(both[:, 0:NE], xT_lo[:, c, ts], wr_split[:, c, 0, :], start=False, stop=c == KC - 1,
                                           skip_group_check=True)
                    mm.then_inc(S["bank"], 1)

                def sum_squares():
                    wait(pe, "h_even", f"{NJ - 2}", it)
                    wait(pe, "sumsq", f"{NJ - 1}", it)
                    if it.n == 0:
                        pe.wait_ge(s_ones, 1)
                    for t in range(NT):
                        mm = pe.matmul(A[1][:, t:t + 1], sumsq[:, t * P:(t + 1) * P], ones[:, 0:1].bitcast(F32), start=True, stop=True)
                    mm.then_inc(S["bank"], 1)

                def comb_transposed():
                    wait(pe, "router", "hi2", it)
                    if nxt:
                        wait(pe, "adj", "epsI", it)
                    elif gnn:
                        wait(pe, "h_odd", f"{NJ - 1}", it)
                    else:
                        wait(pe, "router", "copy", it)
                    for t in range(NT):
                        mm = pe.transpose(A[0][0:3 * NE, t * P:(t + 1) * P], comb_stack[:, t, :].bitcast(F32), ident[:, :])
                    mm.then_inc(S["bank"], 1)

                def adj_transposed():
                    loaded(pe, s_adj, it, lambda i: i + 1, per=1)
                    if gnn:
                        wait(pe, "h_odd", f"{NJ - 1}", it)
                    for b in range(GB):
                        mm = pe.transpose(A[0][:, b * P:(b + 1) * P], adj_in[:, b, :], ident[:, :])
                    mm.then_inc(S["bank"], 1)

                def rms_rows():
                    wait(pe, "rms", "diag_lo", it)
                    pe.matmul(A[1][:, :], ones[:, :], diag_hi, start=True, stop=False)
                    pe.matmul(A[1][:, :], ones[:, :], diag_lo, start=False, stop=True).then_inc(S["bank"], 1)

                def b2_rows(y):
                    if y == 0:
                        wait(pe, "router", "combT", it)
                        if it.n == 1:
                            pe.wait_ge(s_eb2, 5)
                    else:
                        wait(pe, "b2", "0", it)
                    for t in range(2):
                        tt = 2 * y + t
                        mm = pe.matmul(A[0][:, t * D:(t + 1) * D], combT[:, tt * P:(tt + 1) * P], eb2_stack[:, :], start=True, stop=True)
                    mm.then_inc(S["bank"], 1)

                def project(j):
                    wait(pe, "act_lo", f"{j}", it)
                    if j == 0:
                        if prev.has("gnn"):
                            wait(pe, "x2", "1", prev)
                        if it.n == 0:
                            pe.wait_ge(s_wlo, 2)
                    for y in range(2):
                        for t in range(2):
                            ts = slice((2 * y + t) * P, (2 * y + t + 1) * P)
                            mm = three(O[y][:, t * D:(t + 1) * D], act_hi[:, j % NA, ts], act_lo[:, j % NA, ts],
                                       W2_hi[:, j, :], W2_lo[:, j, :], j == 0 and t == 0, j == NJ - 1)
                    mm.then_inc(S["w2"], 1)

                def aggregate():
                    wait(pe, "lo", "xn", it)
                    wait(pe, "lo", "adjT", it)
                    for c in range(KC):
                        if c == 0:
                            if moe:
                                wait(pe, "b2", "1", it)
                        elif gnn:
                            wait(pe, "y", f"{NJ - 1}", it)
                        cs = slice(c * P, (c + 1) * P)
                        for b in range(GB):
                            mm = three(A[c][:, b * P:(b + 1) * P], xn_hi[:, b, cs], xn_lo[:, b, cs], adjT_hi[:, b, :], adjT_lo[:, b, :],
                                       True, True)
                        mm.then_inc(S["bank"], 1)

                def tokens_transposed():
                    for c in range(KC):
                        if nxt:
                            wait(pe, "lo", f"agg{c}", it)
                        elif c == 0:
                            if moe:
                                wait(pe, "b2", "1", it)
                        else:
                            wait(pe, "y", f"{NJ - 1}", it)
                        if c == 0:
                            wait(pe, "ln", f"b_x{NT - 1}", it)
                        for t in range(NT):
                            mm = pe.transpose(A[c][:, t * P:(t + 1) * P], xn[:, t, c * P:(c + 1) * P], ident[:, :])
                        mm.then_inc(S["bank"], 1)

                if moe:
                    logits()
                    if it.n == 1:
                        pe.wait_ge(s_wlo, len(STAGES))
                    expert_hidden(0)
                if gnn:
                    for j in range(NJ // 2):
                        hidden_rows(j)
                if moe:
                    expert_hidden(1)
                if gnn:
                    for j in range(NJ // 2, NJ):
                        hidden_rows(j)
                if moe:
                    expert_out(0)
                    expert_hidden(2)
                if nxt:
                    adj_transposed()
                if moe:
                    expert_out(1)
                    expert_hidden(3, (0,))
                if gnn:
                    sum_squares()
                if moe:
                    expert_hidden(3, (1,))
                    expert_out(2)
                if gnn:
                    rms_rows()
                if moe:
                    expert_hidden(4)
                    comb_transposed()
                    expert_out(3)
                if gnn:
                    for j in range(0, 2):
                        project(j)
                if moe:
                    expert_hidden(5)
                if moe:
                    b2_rows(0)
                if gnn:
                    for j in range(2, 5):
                        project(j)
                if moe:
                    expert_out(4)
                    expert_hidden(6)
                if moe:
                    b2_rows(1)
                if gnn:
                    for j in range(5, NJ):
                        project(j)
                if moe:
                    expert_out(5)
                    expert_hidden(7)
                if nxt:
                    aggregate()
                if moe:
                    expert_out(6)
                if gnn:
                    tokens_transposed()
                if moe:
                    expert_out(7)

            iterations(pe, body)


_INS = ['x', 'adj', 'L0_gnn_epsilon', 'L0_gnn_W1', 'L0_gnn_b1', 'L0_gnn_rms_weight', 'L0_gnn_W2', 'L0_gnn_b2',
        'L0_ffn_router_w', 'L0_ffn_w1', 'L0_ffn_b1', 'L0_ffn_w2', 'L0_ffn_b2']
_OUTS = [((128, 128, 256), 'float32')]


def kernel(**inputs):
    import numpy as _np
    import concourse.bacc as _bacc
    from concourse import mybir as _mybir
    from concourse.bass_utils import run_bass_kernel_spmd as _run

    nc = _bacc.Bacc("TRN2", target_bir_lowering=False, num_devices=1)
    arrays, args = {}, []
    for name in _INS:
        a = _np.ascontiguousarray(inputs[name])
        if a.ndim == 0:
            a = a.reshape(1)
        arrays[f"in_{name}_dram"] = a
        args.append(nc.dram_tensor(f"in_{name}_dram", a.shape, _mybir.dt.from_np(a.dtype), kind="ExternalInput").ap())
    for i, (shape, dtype) in enumerate(_OUTS):
        dt = _mybir.dt.from_np(_np.dtype(dtype))
        args.append(nc.dram_tensor(f"out_{i}_dram", shape, dt, kind="ExternalOutput").ap())
    gnn_moe_kernel(nc, *args)
    r = _run(nc, [arrays], core_ids=[0])
    got = tuple(r.results[0][f"out_{i}_dram"] for i in range(len(_OUTS)))
    return got[0]
```

```python
from contextlib import ExitStack

import concourse.bass as bass
from concourse import mybir


F32 = mybir.dt.float32
F32R = mybir.dt.float32r
U32 = mybir.dt.uint32
ALU = mybir.AluOpType
ACT = mybir.ActivationFunctionType
AX_X = mybir.AxisListType.X

P = 128
LN_EPS = 1e-5
RMS_EPS = 1e-6

def _events(NJ, NE, NT):
    ev = {}
    ev["bank"] = ([("logits", "moe")] + [(f"h{j}", "gnn") for j in range(NJ)]
                  + [("adjT", "next"), ("ss", "gnn"), ("rms", "gnn"),
                     ("combT", "moe"), ("b2_0", "moe"), ("b2_1", "moe"), ("agg00", "next"), ("agg01", "next"),
                     ("agg10", "next"), ("agg11", "next"), ("xT0", "gnn"), ("xT1", "gnn")])
    ev["hidden"] = [(f"{e}_{f}", "moe") for e in range(NE) for f in range(2)]
    ev["expert"] = [(f"{e}_{y}", "moe") for e in range(NE) for y in range(2)]
    ev["w2"] = [(f"{j}", "gnn") for j in range(NJ)]
    ev["gelu"] = [(f"{e}_{f}", "moe") for e in range(NE) for f in range(2)]
    ev["gelu_hi"] = [(f"{e}_{f}", "moe") for e in range(NE) for f in range(2)]
    ev["h_even"] = [(f"{j}", "gnn") for j in range(0, NJ, 2)]
    ev["sq"] = [(f"{j}", "gnn") for j in range(NJ)]
    ev["tanh"] = [(f"{j}", "gnn") for j in range(NJ)]
    ev["act_hi"] = [(f"{j}", "gnn") for j in range(NJ)]
    ev["adj_hi"] = [("adjT", "next")]
    ev["hi"] = [("xn", "next"), ("agg0", "next"), ("agg1", "next"),
                ("xT0", "gnn"), ("xT1", "gnn")]
    ev["ln"] = ([(f"a_st{t}", "next") for t in range(NT)] + [(f"a_ag{t}", "next") for t in range(NT)]
                + [("a_var", "next")] + [(f"a_x{t}", "next") for t in range(NT)]
                + [(f"b_st{t}", "gnn") for t in range(NT)] + [(f"b_ag{t}", "gnn") for t in range(NT)]
                + [("b_var", "gnn")] + [(f"b_x{t}", "gnn") for t in range(NT)])
    ev["router"] = ([(n, "moe") for n in ["copy", "parts", "max", "shift", "sum", "rsum", "prob"]]
                    + [(f"top{t}", "moe") for t in range(NT)] + [(f"idx{t}", "moe") for t in range(NT)]
                    + [(n, "moe") for n in ["cast", "pair", "floor", "rpair", "w", "m0", "m1", "c0", "c1", "comb", "hi", "lo", "hi2", "combT"]])
    ev["lo"] = [("xn", "next"), ("agg0", "next"),
                ("xT0", "gnn"), ("xT1", "gnn"), ("agg1", "next")]
    ev["agg_sum"] = [(f"{c}{g}", "next") for c in range(2) for g in range(2)]
    ev["h_odd"] = [(f"{j}", "gnn") for j in range(1, NJ, 2)]
    ev["adj"] = [("epsI", "next")]
    ev["adj_lo"] = [("adjT", "next")]
    ev["rms"] = [(n, "gnn") for n in ["ms", "hi", "lo", "diag_hi", "diag_lo"]]
    ev["y"] = [(f"{j}", "gnn") for j in range(NJ)]
    ev["silu"] = [(f"{j}", "gnn") for j in range(NJ)]
    ev["act_lo"] = [(f"{j}", "gnn") for j in range(NJ)]
    ev["x2"] = [("0", "gnn"), ("1", "gnn")]
    ev["b2"] = [("0", "moe"), ("1", "moe")]
    ev["acc"] = [(f"{e}_{y}", "moe") for e in range(NE) for y in range(2)]
    ev["pow"] = [("exp0", "moe"), ("a", "next"), ("exp1", "moe"), ("rms", "gnn"), ("b", "gnn")]
    ev["gelu_lo"] = [(f"{e}_{f}", "moe") for e in range(NE) for f in range(2)]
    ev["sumsq"] = [(f"{j}", "gnn") for j in range(1, NJ)]
    ev["xb"] = [("x", "next")]
    ev["acc0"] = [("xn2", "gnn")]
    return ev


def gnn_moe_kernel(nc, x, adj, eps, W1, b1, rms_w, W2, b2, router_w, w1, eb1, w2, eb2, out):
    NB, N, D = x.shape
    H = W1.shape[1]
    NE = router_w.shape[0]
    GB = 4
    T = GB * N
    NG = NB // GB
    NT = T // P
    KC = D // P
    NA = 3
    NJ = H // P
    assert (N, D, T, KC) == (P, 256, 512, 2)
    EV = _events(NJ, NE, NT)
    H_SEM = ["h_even", "h_odd"]

    def parts(i):
        return [n for n, on in (("next", -1 <= i < NG - 1), ("gnn", 0 <= i < NG), ("moe", 1 <= i <= NG)) if on]

    def count(sem, what, i):
        names = [n for n, _ in EV[sem]]
        where = names.index(what)
        part = EV[sem][where][1]
        if part not in parts(i):
            assert i < 2
            return 0
        total = 0
        for j in range(-1, i):
            total += sum(p in parts(j) for _, p in EV[sem])
        return total + sum(p in parts(i) for _, p in EV[sem][:where + 1])

    class Step:

        def __init__(self, n, k=None):
            self.n, self.k = n, k

        def back(self, d):
            return Step(self.n - d, self.k)

        def at(self, f):
            if self.k is None:
                return f(self.n)
            slope = f(self.n + 2) - f(self.n)
            assert f(self.n + 4) - f(self.n + 2) == slope
            return f(self.n) + self.k * slope

        def has(self, part):
            return part in parts(self.n)

    with ExitStack() as ctx:
        def sb(name, shape, dt=F32):
            return ctx.enter_context(nc.sbuf_tensor(name, shape, dt))

        W1_hi, W1_lo = sb("W1_hi", [P, KC, H], F32R), sb("W1_lo", [P, KC, H], F32R)
        W2_hi, W2_lo = sb("W2_hi", [P, NJ, D], F32R), sb("W2_lo", [P, NJ, D], F32R)
        w1_hi, w1_lo = sb("w1_hi", [P, NE, KC, D], F32R), sb("w1_lo", [P, NE, KC, D], F32R)
        w2_hi, w2_lo = sb("w2_hi", [P, NE, KC, D], F32R), sb("w2_lo", [P, NE, KC, D], F32R)
        wr_split = sb("wr_split", [P, KC, 2, NE], F32R)
        ident = sb("ident", [P, P])
        ones = sb("ones", [P, P], F32R)
        neg_half = sb("neg_half", [P, NT])
        e_base = sb("e_base", [P, NT, NE])
        expert_no = sb("expert_no", [P, NE])
        eps_col = sb("eps_col", [P, 1])
        ROWS = 2 * NJ + 2 * KC * NE
        cols = sb("cols", [P, ROWS])
        b1_col = cols[:, 0:NJ]
        rms_w_col = cols[:, NJ:2 * NJ]
        eb1_col = cols[:, 2 * NJ:2 * NJ + KC * NE].rearrange("p (e k) -> p e k", k=KC)
        wr = cols[:, 2 * NJ + KC * NE:ROWS].rearrange("p (k e) -> p k e", k=KC)
        half_w = sb("half_w", [P, NJ])
        b2_row = sb("b2_row", [P, D])
        eb2_stack = sb("eb2_stack", [3 * NE, D], F32R)
        low_row, high_row = sb("low_row", [3 * NE, 1]), sb("high_row", [3 * NE, 1])
        x_in = sb("x_in", [P, 2, GB, D])
        adj_in = sb("adj_in", [P, GB, N])
        acc = sb("acc", [P, 2, NT, D])
        xn = sb("xn", [P, NT, D])
        xn_hi, xn_lo = sb("xn_hi", [P, GB, D], F32R), sb("xn_lo", [P, GB, D], F32R)
        adjT_split = sb("adjT_split", [P, GB, 2, N], F32R)
        agg_hi, agg_lo = sb("agg_hi", [P, KC, T], F32R), sb("agg_lo", [P, KC, T], F32R)
        h = sb("h", [P, NJ, T])
        sq = sb("sq", [P, 2, T])
        agg = h[:, 0:KC, :]
        sumsq = sb("sumsq", [P, T])
        ones_stage = sumsq[:, 0:P]
        tanh = sq
        rows = sq[0:ROWS, 0, 0:P]
        eb2_sb = sq[0:3 * NE, 1, 0:D]
        act_hi, act_lo = sb("act_hi", [P, NA, T], F32R), sb("act_lo", [P, NA, T], F32R)
        diag_hi, diag_lo = act_hi[:, 0, :], act_lo[:, 0, :]
        xT_hi, xT_lo = sb("xT_hi", [P, KC, T], F32R), sb("xT_lo", [P, KC, T], F32R)
        gelu = sb("gelu", [P, 2, T])
        gelu_hi, gelu_lo = sb("gelu_hi", [P, 2, KC, T], F32R), sb("gelu_lo", [P, 2, KC, T], F32R)
        stats = sb("stats", [P, 2, NT, 6])
        mean_var = sb("mean_var", [P, 2, NT, 2])
        var_eps = sb("var_eps", [P, 2, NT])
        rstd = sb("rstd", [P, 2, NT])
        ms_eps = sb("ms_eps", [P, NT])
        rrms = sb("rrms", [P, NT])
        rrms_hi, rrms_lo = sb("rrms_hi", [P, NT], F32R), sb("rrms_lo", [P, NT])
        logit2 = sb("logit2", [P, NT, 2, NE])
        logit = logit2[:, :, 0, :]
        top_logit = sb("top_logit", [P, NT])
        shifted = sb("shifted", [P, NT, NE])
        expd = sb("expd", [P, NT, NE])
        rsum = sb("rsum", [P, 2, NT])
        prob = expd
        top = sb("top", [P, NT, NE])
        top_at = sb("top_at", [P, NT, NE], U32)
        top_at_f = sb("top_at_f", [P, NT, 2])
        pair = sb("pair", [P, 3, NT])
        weight = sb("weight", [P, NT, 2])
        mask = sb("mask", [P, 2, NT, NE])
        comb = sb("comb", [P, NT, NE])
        comb_stack = sb("comb_stack", [P, NT, 3 * NE], F32R)
        combT = sb("combT", [3 * NE, T], F32R)

        def bank(name):
            return ctx.enter_context(nc.psum_tensor(name, [P, 512], F32))

        A = [bank("A0"), bank("A1")]
        O = [bank("O0"), bank("O1")]
        HB = [bank("H0"), bank("H1")]
        Y = [bank("Y0"), bank("Y1")]

        BANK_OF = {"logits": 0, **{f"h{j}": (j + 1) % 2 for j in range(NJ)}, "ss": 1, "combT": 0,
                   "adjT": 0, "rms": 1, "b2_0": 0, "b2_1": 0, **{f"agg{c}{g}": g for c in range(2) for g in range(2)}, "xT0": 0, "xT1": 1}

        S = {name: ctx.enter_context(nc.semaphore(f"s_{name}")) for name in EV}
        s_x = [ctx.enter_context(nc.semaphore(f"s_x{p}")) for p in range(2)]
        s_adj = ctx.enter_context(nc.semaphore("s_adj_in"))
        s_out = [ctx.enter_context(nc.semaphore(f"s_out{p}")) for p in range(2)]
        s_small = ctx.enter_context(nc.semaphore("s_small"))
        s_const = ctx.enter_context(nc.semaphore("s_const"))
        s_stage = [ctx.enter_context(nc.semaphore(f"s_stage{p}")) for p in range(2 + NE)]
        s_whi = ctx.enter_context(nc.semaphore("s_whi"))
        s_wlo = [ctx.enter_context(nc.semaphore(f"s_wlo{n}")) for n in range(2 + NE)]
        s_eps = ctx.enter_context(nc.semaphore("s_eps"))
        s_passed = ctx.enter_context(nc.semaphore("s_passed"))
        s_wr = ctx.enter_context(nc.semaphore("s_wr"))
        s_turned = ctx.enter_context(nc.semaphore("s_turned"))
        s_cols = ctx.enter_context(nc.semaphore("s_cols"))
        s_ones = ctx.enter_context(nc.semaphore("s_ones"))
        s_eb2 = ctx.enter_context(nc.semaphore("s_eb2"))
        s_halfw = ctx.enter_context(nc.semaphore("s_halfw"))

        def wait(eng, sem, what, it):
            v = it.at(lambda i: count(sem, what, i))
            if it.k is None and v <= 0:
                return
            assert it.k is not None or v > 0
            assert count(sem, what, it.n) > 0, (sem, what, it.n)
            eng.wait_ge(S[sem], v)

        def wait_alone(eng, sem, what, it):
            wait(eng, sem, what, it)
            eng.sem_inc(s_passed, 1)

        def loaded(eng, sem, it, g, per=2):
            eng.wait_ge(sem, it.at(lambda i: 16 * (g(i) // per + 1)))

        SMALL = 16 * 9
        CONST = 8

        def gelu_low(eng, it, e):
            prev = it.back(1)
            for f in range(2):
                wait(eng, "gelu_hi", f"{e}_{f}", it)
                if e >= 2:
                    wait(eng, "expert", f"{e - 2}_1", it)
                elif prev.has("moe"):
                    wait(eng, "expert", f"{NE + e - 2}_1", prev)
                eng.tensor_tensor(gelu_lo[:, e % 2, f, :], gelu[:, f, :], gelu_hi[:, e % 2, f, :].bitcast(F32),
                                  ALU.subtract).then_inc(S["gelu_lo"], 1)

        def iterations(eng, body, first=-1):
            for i in range(first, 2):
                body(Step(i))
            with eng.Fori(0, (NG - 4) // 2) as k:
                body(Step(2, k))
                body(Step(3, k))
            for i in range(NG - 2, NG + 1):
                body(Step(i))

        gelu_stage = gelu[:, :, :].rearrange("p f t -> p (f t)")
        acc_stage = acc[:, 1, :, :].rearrange("p t d -> p (t d)")
        STAGES = [
            (h[:, 0:NJ // 2, :].rearrange("p j t -> p (j t)"), W1.rearrange("(k p) h -> p k h", p=P),
             W1_hi[:, :, :].rearrange("p k h -> p (k h)"), W1_lo[:, :, :].rearrange("p k h -> p (k h)")),
            (h[:, NJ // 2:NJ, :].rearrange("p j t -> p (j t)"), W2.rearrange("(j p) d -> p j d", p=P),
             W2_hi[:, :, :].rearrange("p j d -> p (j d)"), W2_lo[:, :, :].rearrange("p j d -> p (j d)")),
        ]
        for w, hi, lo in ((w1, w1_hi, w1_lo), (w2, w2_hi, w2_lo)):
            for e in range(0, NE, 2):
                STAGES.append(([gelu_stage, acc_stage][(e // 2) % 2],
                               w[e:e + 2].rearrange("e (k p) f -> p (e k) f", p=P),
                               hi[:, e:e + 2, :, :].rearrange("p e k f -> p (e k f)"),
                               lo[:, e:e + 2, :, :].rearrange("p e k f -> p (e k f)")))
        LOW_BY_VECTOR = (0, 4, 5)

        def split_high(act, n):
            src, _, hi, _ = STAGES[n]
            act.wait_ge(s_stage[n], 16)
            act.activation(hi, src, ACT.Copy).then_inc(s_whi, 1)

        def split_low(eng, n):
            assert (eng is nc.vector) == (n in LOW_BY_VECTOR)
            src, _, hi, lo = STAGES[n]
            eng.wait_ge(s_whi, n + 1)
            eng.tensor_tensor(lo, src, hi.bitcast(F32), ALU.subtract).then_inc(s_wlo[n], 1)

        block = ctx.enter_context(nc.Block())

        @block.sync
        def _(sp):
            def load_x(it, g, p):
                sp.dma_start(x_in[:, p, :, :], x[bass.ds(g * GB, GB), :, :].rearrange("b n d -> n b d")).then_inc(s_x[p], 16)

            def load_adj(it, g):
                sp.dma_start(adj_in[:, :, :], adj[bass.ds(g * GB, GB), :, :].rearrange("b n m -> n b m")).then_inc(s_adj, 16)

            def store(it, g, p):
                wait(sp, "acc", f"{NE - 1}_1", it)
                sp.dma_start(out[bass.ds(g * GB, GB), :, :].rearrange("b n d -> n b d"), acc[:, p, :, :]).then_inc(s_out[p], 16)

            def stage(n):
                dst, src, _, _ = STAGES[n]
                if n >= 4:
                    sp.wait_ge(s_wlo[n - 2], 1)
                sp.dma_start(dst.rearrange("p (a b) -> p a b", b=src.shape[2]), src).then_inc(s_stage[n], 16)

            load_x(None, 0, 0)
            load_adj(None, 0)
            stage(0)
            load_x(None, 1, 1)
            stage(1)
            stage(2)
            stage(3)
            wait(sp, "adj_lo", "adjT", Step(-1))
            load_adj(None, 1)
            for n in range(4, len(STAGES)):
                stage(n)

            def body(it, g, p):
                wait(sp, "adj_lo", "adjT", it)
                load_adj(it, g)
                wait(sp, "x2", "1", it)
                load_x(it, g, p)
                if it.has("moe"):
                    store(it, g - 3, 1 - p)

            body(Step(0), 2, 0)
            body(Step(1), 3, 1)
            with sp.Fori(0, (NG - 4) // 2) as k:
                body(Step(2, k), k * 2 + 4, 0)
                body(Step(3, k), k * 2 + 5, 1)
            for i in range(NG - 2, NG + 1):
                store(Step(i), i - 1, (i - 1) % 2)
            sp.wait_ge(s_out[0], 16 * (NG // 2))
            sp.wait_ge(s_out[1], 16 * (NG // 2))

        @block.gpsimd
        def _(pool):
            pool.memset(ident[:, :], 0.0).then_inc(s_const, 1)
            pool.memset(ones_stage, 1.0).then_inc(s_const, 1)
            pool.memset(neg_half[:, :], -0.5).then_inc(s_const, 1)
            pool.memset(e_base[:, :, :], 2.718281828459045).then_inc(s_const, 1)
            pool.iota(expert_no[:, :], [[1, NE]], base=0, channel_multiplier=0,
                      allow_small_or_imprecise_dtypes=True).then_inc(s_const, 1)
            pool.memset(low_row[:, :], 1.0).then_inc(s_const, 1)
            pool.wait_ge(s_const, 6)
            pool.affine_select(out=low_row[:, :], in_=low_row[:, :], compare_op=ALU.is_ge, fill=0.0, base=-2 * NE,
                               pattern=[[0, 1]], channel_multiplier=1).then_inc(s_const, 1)
            pool.affine_select(out=ident[:, :], in_=ident[:, :], compare_op=ALU.not_equal, fill=1.0, base=0,
                               pattern=[[-1, P]], channel_multiplier=1).then_inc(s_const, 1)
            pool.wait_ge(s_const, CONST)

            def body(it):
                prev = it.back(1)
                moe, gnn, nxt = it.has("moe"), it.has("gnn"), it.has("next")
                p = it.n % 2

                def add_square(j):
                    wait(pool, "sq", f"{j}", it)
                    if j == 1:
                        if prev.has("gnn"):
                            wait(pool, "bank", "rms", prev)
                        else:
                            pool.wait_ge(s_ones, 1)
                        pool.tensor_tensor(sumsq[:, :], sq[:, 0, :], sq[:, 1, :], ALU.add).then_inc(S["sumsq"], 1)
                    elif j > 1:
                        wait(pool, "sumsq", f"{j - 1}", it)
                        pool.tensor_tensor(sumsq[:, :], sumsq[:, :], sq[:, j % 2, :], ALU.add).then_inc(S["sumsq"], 1)

                def exponentials(half):
                    if half == 0:
                        wait(pool, "router", "shift", it)
                    ts = slice(2 * half, 2 * half + 2)
                    pool.tensor_tensor(expd[:, ts, :], e_base[:, ts, :], shifted[:, ts, :], ALU.pow).then_inc(S["pow"], 1)

                if moe:
                    exponentials(0)
                if nxt:
                    wait(pool, "ln", "a_var", it)
                    pool.tensor_tensor(rstd[:, 0, :], var_eps[:, 0, :], neg_half[:, :], ALU.pow).then_inc(S["pow"], 1)
                if moe and gnn:
                    gelu_low(pool, it, 0)
                if moe:
                    exponentials(1)
                if gnn:
                    add_square(1)
                if moe and gnn:
                    gelu_low(pool, it, 1)
                if gnn:
                    for j in range(2, NJ):
                        add_square(j)
                if moe:
                    if not gnn:
                        wait(pool, "gelu_hi", "2_1", it)
                    gelu_low(pool, it, 2)
                if gnn:
                    wait(pool, "rms", "ms", it)
                    pool.tensor_tensor(rrms[:, :], ms_eps[:, :], neg_half[:, :], ALU.pow).then_inc(S["pow"], 1)
                if moe:
                    for e in range(3, 6):
                        gelu_low(pool, it, e)
                if nxt:
                    wait(pool, "ln", f"a_x{NT - 1}", it)
                    if it.n == -1:
                        pool.wait_ge(s_small, SMALL)
                    pool.tensor_tensor(x_in[:, 1 - p, :, :], x_in[:, 1 - p, :, :],
                                       b2_row[:, :].unsqueeze(1).broadcast_to([P, GB, D]), ALU.add).then_inc(S["xb"], 1)
                if it.n == 0:
                    for n in range(6, 2 + NE):
                        split_low(pool, n)
                if moe:
                    gelu_low(pool, it, 6)
                if gnn:
                    wait(pool, "ln", "b_var", it)
                    pool.tensor_tensor(rstd[:, 1, :], var_eps[:, 1, :], neg_half[:, :], ALU.pow).then_inc(S["pow"], 1)
                if moe:
                    gelu_low(pool, it, 7)
                if gnn:
                    wait(pool, "ln", f"b_x{NT - 1}", it)
                    pool.tensor_tensor(acc[:, p, :, :], acc[:, p, :, :], xn[:, :, :], ALU.add).then_inc(S["acc0"], 1)

            body(Step(-1))
            for n in range(1, 4):
                split_low(pool, n)
            iterations(pool, body, 0)

        @block.scalar
        def _(act):
            act.dma_start(eps_col[:, :], eps.partition_broadcast(P)).then_inc(s_eps, 16)
            act.dma_start(rows[0:NJ], b1.rearrange("(j p) -> j p", p=P)).then_inc(s_small, 16)
            act.dma_start(rows[NJ:2 * NJ], rms_w.rearrange("(j p) -> j p", p=P)).then_inc(s_small, 16)
            r0 = 2 * NJ
            act.dma_start(rows[r0:r0 + KC * NE], eb1.rearrange("e (k p) -> (e k) p", p=P)).then_inc(s_small, 16)
            for kc in range(KC):
                r0 = 2 * NJ + KC * NE + kc * NE
                act.dma_start(rows[r0:r0 + NE], router_w[:, kc * P:(kc + 1) * P]).then_inc(s_small, 16)
            for s in range(3):
                act.dma_start(sq[s * NE:(s + 1) * NE, 1, 0:D], eb2).then_inc(s_small, 16)
            act.dma_start(b2_row[:, :], b2.partition_broadcast(P)).then_inc(s_small, 16)

            def body(it):
                prev = it.back(1)
                moe, gnn, nxt = it.has("moe"), it.has("gnn"), it.has("next")

                def gelu_row(e, f):
                    wait(act, "hidden", f"{e}_{f}", it)
                    if e >= 1:
                        wait(act, "gelu_lo", f"{e - 1}_{f}", it)
                    elif prev.has("moe"):
                        wait(act, "gelu_lo", f"{NE - 1}_{f}", prev)
                    act.activation(gelu[:, f, :], HB[f][:, :], ACT.Gelu,
                                   bias=eb1_col[:, e, f:f + 1]).then_inc(S["gelu"], 1)

                def high_row(e, f):
                    wait(act, "gelu", f"{e}_{f}", it)
                    if e >= 2:
                        wait(act, "expert", f"{e - 2}_1", it)
                    elif prev.has("moe"):
                        wait(act, "expert", f"{NE + e - 2}_1", prev)
                    act.activation(gelu_hi[:, e % 2, f, :], gelu[:, f, :], ACT.Copy).then_inc(S["gelu_hi"], 1)

                apart = (0, 1, 2, 4, 5) if gnn else ()

                def gelus(e):
                    for f in range(2):
                        gelu_row(e, f)
                        if e not in apart:
                            high_row(e, f)

                def gelu_high(e):
                    if e in apart:
                        for f in range(2):
                            high_row(e, f)

                def hidden_rows(j):
                    wait(act, "bank", f"h{j}", it)
                    if prev.has("gnn"):
                        wait(act, "act_lo", f"{j}", prev)
                    if j < KC:
                        wait(act, "lo", f"agg{j}", prev)
                    elif it.n == 0:
                        act.wait_ge(s_wlo[2 * j // NJ], 1)
                    act.activation(h[:, j, :], A[BANK_OF[f"h{j}"]][:, :], ACT.Identity,
                                   bias=b1_col[:, j:j + 1]).then_inc(S["h_even"], 1)

                def squares(a, b):
                    for j in range(a, b):
                        wait(act, H_SEM[j % 2], f"{j}", it)
                        if j == 2:
                            wait(act, "sumsq", "1", it)
                        elif j > 2:
                            wait(act, "sumsq", f"{j - 2}", it)
                        elif prev.has("gnn"):
                            wait(act, "silu", f"{NJ - 2 + j}", prev)
                        act.activation(sq[:, j % 2, :], h[:, j, :], ACT.Square).then_inc(S["sq"], 1)

                def tanhs(a, b):
                    for j in range(a, b):
                        wait(act, "y", f"{j}", it)
                        if j >= 2:
                            wait(act, "silu", f"{j - 2}", it)
                        else:
                            wait(act, "sumsq", f"{NJ - 1}", it)
                        act.activation(tanh[:, j % 2, :], h[:, j, :], ACT.Tanh).then_inc(S["tanh"], 1)

                def silu_high(a, b):
                    for j in range(a, b):
                        wait(act, "silu", f"{j}", it)
                        if j >= NA:
                            wait(act, "w2", f"{j - NA}", it)
                        elif prev.has("gnn"):
                            wait(act, "w2", f"{NJ - 1}", prev)
                        act.activation(act_hi[:, j % NA, :], h[:, j, :], ACT.Copy).then_inc(S["act_hi"], 1)

                def stages(i, *numbers):
                    if it.n == i:
                        for n in numbers:
                            split_high(act, n)

                def adjacency_high():
                    wait(act, "adj", "epsI", it)
                    act.activation(adjT_split[:, :, 0, :], adj_in[:, :, :], ACT.Copy).then_inc(S["adj_hi"], 1)

                if moe:
                    gelus(0)
                if gnn:
                    hidden_rows(0)
                if moe:
                    gelu_high(0)
                if gnn and not moe:
                    squares(0, 2)
                    hidden_rows(2)
                    squares(2, 4)
                    hidden_rows(4)
                    squares(4, 6)
                    hidden_rows(6)
                    squares(6, 8)
                if gnn and moe:
                    hidden_rows(2)
                    squares(0, 2)
                if moe:
                    gelus(1)
                if gnn and moe:
                    hidden_rows(4)
                    squares(2, 3)
                if moe:
                    gelu_high(1)
                if gnn and moe:
                    hidden_rows(6)
                    squares(3, 4)
                if it.n == -1:
                    adjacency_high()
                if nxt:
                    wait(act, "ln", f"a_x{NT - 1}", it)
                    if prev.has("next"):
                        wait(act, "bank", "agg11", prev)
                    act.activation(xn_hi[:, :, :], xn[:, :, :], ACT.Copy).then_inc(S["hi"], 1)
                stages(-1, 0)
                if gnn and moe:
                    squares(4, 7)
                if moe:
                    gelus(2)
                if gnn and moe:
                    squares(7, 8)
                if moe:
                    gelu_high(2)
                if nxt and it.n != -1:
                    adjacency_high()
                stages(-1, 1)
                stages(0, 4, 5)
                if moe:
                    gelus(3)
                if gnn:
                    tanhs(0, 2)
                    silu_high(0, 2)
                stages(0, 6)
                if moe:
                    gelus(4)
                if gnn:
                    tanhs(2, 4)
                    silu_high(2, 3)
                stages(0, 7)
                if moe:
                    gelu_high(4)
                if gnn:
                    tanhs(4, 6)
                    silu_high(3, 5)
                if moe:
                    gelus(5)
                if gnn:
                    tanhs(6, 8)
                if moe:
                    gelu_high(5)
                if gnn:
                    silu_high(5, 8)
                stages(0, 8, 9)
                if moe:
                    gelus(6)
                if moe:
                    gelus(7)
                if nxt:
                    for c in range(KC):
                        wait(act, "agg_sum", f"{c}1", it)
                        act.activation(agg_hi[:, c, :], agg[:, c, :], ACT.Copy).then_inc(S["hi"], 1)
                if gnn:
                    for c in range(KC):
                        wait(act, "bank", f"xT{c}", it)
                        act.activation(xT_hi[:, c, :], A[BANK_OF[f"xT{c}"]][:, :], ACT.Copy).then_inc(S["hi"], 1)

            act.wait_ge(s_const, CONST)
            act.activation(top_logit[:, :], neg_half[:, :], ACT.Copy).then_inc(s_const, 1)
            body(Step(-1))
            for n in range(2, 4):
                split_high(act, n)
            act.wait_ge(s_cols, 1)
            iterations(act, body, 0)

        @block.vector
        def _(dve):
            dve.wait_ge(s_const, CONST)
            dve.tensor_copy(ones[:, :], ones_stage).then_inc(s_ones, 1)
            def body(it):
                prev = it.back(1)
                moe, gnn, nxt = it.has("moe"), it.has("gnn"), it.has("next")
                p = it.n % 2
                q = 1 - p

                def norm_stats(which, part, src):
                    for t in range(NT):
                        dve.bn_stats(stats[:, part, t, :], src[:, t, :]).then_inc(S["ln"], 1)
                    wait_alone(dve, "ln", f"{which}_st{NT - 1}", it)
                    for t in range(NT):
                        dve.bn_aggr(mean_var[:, part, t, :], stats[:, part, t, :]).then_inc(S["ln"], 1)
                    wait(dve, "ln", f"{which}_ag{NT - 1}", it)
                    dve.tensor_scalar(var_eps[:, part, :], mean_var[:, part, :, 1], LN_EPS, None,
                                      ALU.add).then_inc(S["ln"], 1)

                def norm_apply(which, part, src):
                    wait(dve, "pow", which, it)
                    for t in range(NT):
                        dve.tensor_scalar(xn[:, t, :], src[:, t, :], mean_var[:, part, t, 0:1], rstd[:, part, t:t + 1],
                                          ALU.subtract, ALU.mult).then_inc(S["ln"], 1)

                def router_shift():
                    wait(dve, "bank", "logits", it)
                    dve.tensor_copy(logit2[:, :, :, :], A[0][:, 0:2 * NT * NE].rearrange("p (t s e) -> p t s e", t=NT, s=2)).then_inc(S["router"], 1)
                    wait(dve, "router", "copy", it)
                    dve.tensor_tensor(logit, logit2[:, :, 0, :], logit2[:, :, 1, :], ALU.add).then_inc(S["router"], 1)
                    wait(dve, "router", "parts", it)
                    dve.tensor_reduce(top_logit[:, :], logit, AX_X, ALU.max).then_inc(S["router"], 1)
                    wait(dve, "router", "max", it)
                    if prev.has("moe"):
                        wait(dve, "pow", "exp1", prev)
                    dve.tensor_tensor(shifted[:, :, :], logit, top_logit[:, :].unsqueeze(2).broadcast_to([P, NT, NE]),
                                      ALU.subtract).then_inc(S["router"], 1)

                def router_top():
                    wait(dve, "pow", "exp1", it)
                    dve.tensor_reduce(rsum[:, 0, :], expd[:, :, :], AX_X, ALU.add).then_inc(S["router"], 1)
                    wait(dve, "router", "sum", it)
                    dve.reciprocal(rsum[:, 1, :], rsum[:, 0, :]).then_inc(S["router"], 1)
                    wait(dve, "router", "rsum", it)
                    dve.tensor_tensor(prob[:, :, :], expd[:, :, :], rsum[:, 1, :].unsqueeze(2).broadcast_to([P, NT, NE]),
                                      ALU.mult).then_inc(S["router"], 1)
                    wait_alone(dve, "router", "prob", it)
                    for t in range(NT):
                        dve.max(top[:, t, :], prob[:, t, :]).then_inc(S["router"], 1)
                    wait_alone(dve, "router", f"top{NT - 1}", it)
                    for t in range(NT):
                        dve.max_index(top_at[:, t, :], top[:, t, :], prob[:, t, :]).then_inc(S["router"], 1)
                    wait(dve, "router", f"idx{NT - 1}", it)
                    dve.tensor_copy(top_at_f[:, :, :], top_at[:, :, 0:2]).then_inc(S["router"], 1)

                def router_combine():
                    dve.tensor_tensor(pair[:, 0, :], top[:, :, 0], top[:, :, 1], ALU.add).then_inc(S["router"], 1)
                    wait(dve, "router", "pair", it)
                    dve.tensor_scalar(pair[:, 1, :], pair[:, 0, :], 1e-12, None, ALU.max).then_inc(S["router"], 1)
                    wait(dve, "router", "floor", it)
                    dve.reciprocal(pair[:, 2, :], pair[:, 1, :]).then_inc(S["router"], 1)
                    wait(dve, "router", "rpair", it)
                    dve.tensor_tensor(weight[:, :, :], top[:, :, 0:2], pair[:, 2, :].unsqueeze(2).broadcast_to([P, NT, 2]),
                                      ALU.mult).then_inc(S["router"], 1)
                    for m in range(2):
                        dve.tensor_tensor(mask[:, m, :, :], expert_no[:, :].unsqueeze(1).broadcast_to([P, NT, NE]),
                                          top_at_f[:, :, m:m + 1].broadcast_to([P, NT, NE]), ALU.is_equal).then_inc(S["router"], 1)
                    for m in range(2):
                        wait(dve, "router", f"m{m}", it)
                        dve.tensor_tensor(mask[:, m, :, :], mask[:, m, :, :], weight[:, :, m:m + 1].broadcast_to([P, NT, NE]),
                                          ALU.mult).then_inc(S["router"], 1)
                    wait(dve, "router", "c1", it)
                    if prev.has("moe"):
                        wait(dve, "bank", "combT", prev)
                        wait(dve, "acc", f"{NE - 1}_1", prev)
                    dve.tensor_tensor(comb[:, :, :], mask[:, 0, :, :], mask[:, 1, :, :], ALU.add).then_inc(S["router"], 1)
                    wait(dve, "router", "comb", it)
                    dve.tensor_copy(comb_stack[:, :, 0:NE], comb[:, :, :]).then_inc(S["router"], 1)
                    wait(dve, "router", "hi", it)
                    dve.tensor_tensor(comb_stack[:, :, NE:2 * NE], comb[:, :, :], comb_stack[:, :, 0:NE].bitcast(F32),
                                      ALU.subtract).then_inc(S["router"], 1)
                    dve.tensor_copy(comb_stack[:, :, 2 * NE:3 * NE], comb_stack[:, :, 0:NE].bitcast(F32)).then_inc(S["router"], 1)

                def expert_sum(e):
                    if e == 0:
                        wait(dve, "router", "comb", it)
                        wait(dve, "acc0", "xn2", prev)
                    else:
                        wait(dve, "acc", f"{e - 1}_1", it)
                    if e in (4, 5):
                        wait(dve, "b2", f"{e - 4}", it)
                    for y in range(2):
                        wait(dve, "expert", f"{e}_{y}", it)
                        for t in range(2):
                            tt = 2 * y + t
                            last = dve.scalar_tensor_tensor(out=acc[:, q, tt, :], in0=Y[y][:, t * D:(t + 1) * D],
                                                            scalar=comb[:, tt, e:e + 1], in1=acc[:, q, tt, :],
                                                            op0=ALU.mult, op1=ALU.add)
                        last.then_inc(S["acc"], 1)

                def y_row(j):
                    if j == 0:
                        wait(dve, "bank", "rms", it)
                    wait(dve, H_SEM[j % 2], f"{j}", it)
                    dve.scalar_tensor_tensor(out=h[:, j, :], in0=h[:, j, :], scalar=half_w[:, j:j + 1], in1=A[1][:, :],
                                             op0=ALU.mult, op1=ALU.mult).then_inc(S["y"], 1)

                def silu_rows(a, b):
                    for j in range(a, b):
                        wait(dve, "tanh", f"{j}", it)
                        dve.scalar_tensor_tensor(out=h[:, j, :], in0=tanh[:, j % 2, :], scalar=1.0, in1=h[:, j, :],
                                                 op0=ALU.add, op1=ALU.mult).then_inc(S["silu"], 1)

                def silu_low(a, b):
                    for j in range(a, b):
                        wait(dve, "act_hi", f"{j}", it)
                        dve.tensor_tensor(act_lo[:, j % NA, :], h[:, j, :], act_hi[:, j % NA, :].bitcast(F32),
                                          ALU.subtract).then_inc(S["act_lo"], 1)

                def add_b2(y):
                    wait(dve, "bank", f"b2_{y}", it)
                    wait(dve, "acc", f"{3 + y}_1", it)
                    a = acc[:, q, 2 * y:2 * y + 2, :].rearrange("p t d -> p (t d)")
                    dve.tensor_tensor(a, A[BANK_OF[f"b2_{y}"]][:, :], a, ALU.add).then_inc(S["b2"], 1)

                def aggregate_sum(c):
                    for g in range(2):
                        if c == 0 and g == 0:
                            if it.n == -1:
                                dve.wait_ge(s_wlo[0], 1)
                            elif gnn:
                                wait(dve, "act_lo", f"{NJ - 1}", it)
                        wait(dve, "bank", f"agg{c}{g}", it)
                        dve.tensor_reduce(agg[:, c, 2 * g * N:2 * (g + 1) * N].rearrange("p (b n) -> p b n", b=2),
                                          A[g][:, :].rearrange("p (b s n) -> p b n s", b=2, s=2), AX_X,
                                          ALU.add).then_inc(S["agg_sum"], 1)

                def aggregate_low(c):
                    wait(dve, "hi", f"agg{c}", it)
                    dve.tensor_tensor(agg_lo[:, c, :], agg[:, c, :], agg_hi[:, c, :].bitcast(F32), ALU.subtract).then_inc(S["lo"], 1)

                def low_of_bank(name, lo, hi):
                    wait(dve, "hi", name, it)
                    dve.tensor_tensor(lo, A[BANK_OF[name]][:, :], hi.bitcast(F32), ALU.subtract).then_inc(S["lo"], 1)

                def hidden_rows(j):
                    wait(dve, "bank", f"h{j}", it)
                    if prev.has("gnn"):
                        wait(dve, "act_lo", f"{j}", prev)
                    if j < KC:
                        wait(dve, "lo", f"agg{j}", prev)
                    elif it.n == 0:
                        dve.wait_ge(s_wlo[2 * j // NJ], 1)
                    dve.tensor_scalar(h[:, j, :], A[BANK_OF[f"h{j}"]][:, :], b1_col[:, j:j + 1], None,
                                      ALU.add).then_inc(S["h_odd"], 1)

                def stages(i, *numbers):
                    if it.n == i:
                        for n in numbers:
                            split_low(dve, n)

                def adjacency_eps():
                    wait(dve, "bank", "adjT", it)
                    if it.n == -1:
                        dve.wait_ge(s_eps, 16)
                    dve.scalar_tensor_tensor(out=adj_in[:, :, :], in0=ident[:, :].unsqueeze(1).broadcast_to([P, GB, N]),
                                             scalar=eps_col[:, 0:1], in1=A[0][:, :].rearrange("p (b n) -> p b n", b=GB),
                                             op0=ALU.mult, op1=ALU.add).then_inc(S["adj"], 1)

                def adjacency_low():
                    wait(dve, "adj_hi", "adjT", it)
                    dve.tensor_tensor(adjT_split[:, :, 1, :], adj_in[:, :, :], adjT_split[:, :, 0, :].bitcast(F32),
                                      ALU.subtract).then_inc(S["adj_lo"], 1)

                if moe:
                    router_shift()
                if nxt:
                    loaded(dve, s_x[q], it, lambda i: i + 1)
                    norm_stats("a", 0, x_in[:, q])
                if gnn:
                    hidden_rows(1)
                if nxt:
                    if prev.has("gnn"):
                        wait(dve, "acc0", "xn2", prev)
                    elif prev.has("next"):
                        wait(dve, "lo", "xn", prev)
                    if it.n == -1:
                        adjacency_eps()
                    norm_apply("a", 0, x_in[:, q])
                    if it.n == -1:
                        adjacency_low()
                if gnn:
                    hidden_rows(3)
                if moe and not gnn:
                    gelu_low(dve, it, 0)
                    gelu_low(dve, it, 1)
                if moe:
                    router_top()
                if gnn:
                    hidden_rows(5)
                if moe:
                    router_combine()
                if gnn:
                    hidden_rows(7)
                if moe:
                    expert_sum(0)
                if nxt:
                    wait(dve, "hi", "xn", it)
                    dve.tensor_tensor(xn_lo[:, :, :], xn[:, :, :], xn_hi[:, :, :].bitcast(F32), ALU.subtract).then_inc(S["lo"], 1)
                if nxt and it.n != -1:
                    adjacency_eps()
                if moe:
                    expert_sum(1)
                if nxt and it.n != -1:
                    adjacency_low()
                stages(-1, 0)
                if gnn:
                    wait(dve, "bank", "ss", it)
                    dve.tensor_scalar(ms_eps[:, :], A[1][:, 0:NT], 1.0 / H, RMS_EPS, ALU.mult, ALU.add).then_inc(S["rms"], 1)
                stages(0, 4)
                if gnn:
                    wait(dve, "pow", "rms", it)
                    dve.tensor_copy(rrms_hi[:, :], rrms[:, :]).then_inc(S["rms"], 1)
                    wait(dve, "rms", "hi", it)
                    dve.tensor_tensor(rrms_lo[:, :], rrms[:, :], rrms_hi[:, :].bitcast(F32), ALU.subtract).then_inc(S["rms"], 1)
                    for diag, part, dep in ((diag_hi, rrms_hi[:, :].bitcast(F32), "hi"), (diag_lo, rrms_lo[:, :], "lo")):
                        wait(dve, "rms", dep, it)
                        dve.tensor_tensor(diag.rearrange("p (t n) -> p t n", t=NT), ident[:, :].unsqueeze(1).broadcast_to([P, NT, P]),
                                          part.unsqueeze(2).broadcast_to([P, NT, P]), ALU.mult).then_inc(S["rms"], 1)
                stages(0, 5)
                if moe:
                    expert_sum(2)
                if gnn:
                    y_row(0)
                    y_row(1)
                    silu_rows(0, 2)
                    y_row(2)
                    y_row(3)
                    silu_low(0, 2)
                if gnn:
                    silu_rows(2, 3)
                    y_row(4)
                    y_row(5)
                    silu_rows(3, 4)
                    silu_low(2, 3)
                    y_row(6)
                    y_row(7)
                if moe:
                    wait(dve, "bank", "combT", it)
                    dve.tensor_copy(combT[:, :], A[0][0:3 * NE, :]).then_inc(S["router"], 1)
                if gnn:
                    silu_rows(4, 5)
                    silu_low(3, 4)
                if moe:
                    expert_sum(3)
                if gnn:
                    silu_rows(5, 6)
                    silu_low(4, 5)
                    silu_rows(6, 8)
                    silu_low(5, 7)
                if moe:
                    add_b2(0)
                    expert_sum(4)
                if gnn:
                    silu_low(7, 8)
                if moe:
                    add_b2(1)
                if gnn:
                    wait(dve, "w2", f"{NJ - 1}", it)
                    wait(dve, "xb", "x", prev)
                    if it.n >= 2:
                        dve.wait_ge(s_out[p], it.at(lambda i: 16 * (i // 2)))
                    for y in range(2):
                        dve.tensor_tensor(acc[:, p, 2 * y:2 * y + 2, :].rearrange("p t d -> p (t d)"), O[y][:, :],
                                          x_in[:, p, 2 * y:2 * y + 2, :].rearrange("p t d -> p (t d)"),
                                          ALU.add).then_inc(S["x2"], 1)
                if gnn:
                    wait(dve, "x2", "1", it)
                    norm_stats("b", 1, acc[:, p])
                if nxt:
                    aggregate_sum(0)
                if moe:
                    expert_sum(5)
                if gnn:
                    if nxt:
                        wait(dve, "lo", "xn", it)
                    norm_apply("b", 1, acc[:, p])
                if nxt:
                    aggregate_sum(1)
                if moe:
                    expert_sum(6)
                if nxt:
                    aggregate_low(0)
                if gnn:
                    for c in range(KC):
                        low_of_bank(f"xT{c}", xT_lo[:, c, :], xT_hi[:, c, :])
                if nxt:
                    aggregate_low(1)
                if moe:
                    expert_sum(7)

            body(Step(-1))
            dve.wait_ge(s_turned, 1)
            dve.tensor_copy(cols[:, :], Y[0][:, 0:ROWS]).then_inc(s_cols, 1)
            dve.wait_ge(s_cols, 1)
            dve.tensor_copy(wr_split[:, :, 0, :], wr).then_inc(s_wr, 1)
            dve.wait_ge(s_wr, 1)
            dve.tensor_tensor(wr_split[:, :, 1, :], wr, wr_split[:, :, 0, :].bitcast(F32), ALU.subtract).then_inc(s_wr, 1)
            dve.tensor_copy(eb2_stack[:, :], eb2_sb).then_inc(s_eb2, 1)
            dve.wait_ge(s_eb2, 1)
            dve.tensor_tensor(eb2_sb, eb2_sb, eb2_stack[:, :].bitcast(F32), ALU.subtract).then_inc(s_eb2, 1)
            dve.wait_ge(s_eb2, 2)
            dve.tensor_scalar(eb2_sb, eb2_sb, low_row[:, 0:1], None, ALU.mult).then_inc(s_eb2, 1)
            dve.tensor_scalar(high_row[:, :], low_row[:, :], 1.0, -1.0, ALU.subtract, ALU.mult).then_inc(s_eb2, 1)
            dve.wait_ge(s_eb2, 4)
            dve.scalar_tensor_tensor(out=eb2_stack[:, :], in0=eb2_stack[:, :].bitcast(F32), scalar=high_row[:, 0:1],
                                     in1=eb2_sb, op0=ALU.mult, op1=ALU.add).then_inc(s_eb2, 1)
            dve.tensor_scalar(half_w[:, :], rms_w_col, 0.5, None, ALU.mult).then_inc(s_halfw, 1)
            dve.wait_ge(s_halfw, 1)
            iterations(dve, body, 0)

        @block.tensor
        def _(pe):
            pe.wait_ge(s_const, CONST)
            def three(dst, hi, lo, m_hi, m_lo, start, stop):
                pe.matmul(dst, hi, m_hi, start=start, stop=False, skip_group_check=True)
                pe.matmul(dst, hi, m_lo, start=False, stop=False, skip_group_check=True)
                return pe.matmul(dst, lo, m_hi, start=False, stop=stop, skip_group_check=True)

            def body(it):
                prev = it.back(1)
                moe, gnn, nxt = it.has("moe"), it.has("gnn"), it.has("next")

                def expert_hidden(e, fs=(0, 1)):
                    for f in fs:
                        if e >= 1:
                            wait(pe, "gelu", f"{e - 1}_{f}", it)
                        elif prev.has("moe"):
                            wait(pe, "gelu", f"{NE - 1}_{f}", prev)
                        if e == 0 and f == 0:
                            wait(pe, "lo", "xT1", prev)
                        for c in range(KC):
                            cols_f = slice(f * P, (f + 1) * P)
                            mm = three(HB[f][:, :], w1_hi[:, e, c, cols_f], w1_lo[:, e, c, cols_f], xT_hi[:, c, :], xT_lo[:, c, :],
                                       c == 0, c == KC - 1)
                        mm.then_inc(S["hidden"], 1)

                def expert_out(e):
                    for f in range(2):
                        wait(pe, "gelu_lo", f"{e}_{f}", it)
                    for y in range(2):
                        if e >= 1:
                            wait(pe, "acc", f"{e - 1}_{y}", it)
                        elif prev.has("moe"):
                            wait(pe, "acc", f"{NE - 1}_{y}", prev)
                        for t in range(2):
                            ts = slice((2 * y + t) * P, (2 * y + t + 1) * P)
                            for f in range(2):
                                mm = three(Y[y][:, t * D:(t + 1) * D], gelu_hi[:, e % 2, f, ts], gelu_lo[:, e % 2, f, ts],
                                           w2_hi[:, e, f, :], w2_lo[:, e, f, :], f == 0, f == 1)
                        mm.then_inc(S["expert"], 1)

                def hidden_rows(j):
                    if j == 0:
                        wait(pe, "lo", "xT1", prev)
                        wait(pe, "lo", "agg1", prev)
                        if it.n == 0:
                            pe.wait_ge(s_wlo[0], 1)
                    elif j == 1:
                        if moe:
                            wait(pe, "router", "copy", it)
                        else:
                            wait(pe, "lo", "agg0", prev)
                    else:
                        wait(pe, H_SEM[j % 2], f"{j - 2}", it)
                    js = slice(j * P, (j + 1) * P)
                    for c in range(KC):
                        mm = three(A[BANK_OF[f"h{j}"]][:, :], W1_hi[:, c, js], W1_lo[:, c, js], agg_hi[:, c, :], agg_lo[:, c, :],
                                   c == 0, c == KC - 1)
                    mm.then_inc(S["bank"], 1)

                def logits():
                    wait(pe, "lo", "xT1", prev)
                    if it.n == 1:
                        pe.wait_ge(s_wr, 2)
                    for t in range(NT):
                        both = A[0][:, 2 * t * NE:2 * (t + 1) * NE]
                        ts = slice(t * P, (t + 1) * P)
                        for c in range(KC):
                            w_both = wr_split[:, c, :, :].rearrange("p s e -> p (s e)")
                            pe.matmul(both, xT_hi[:, c, ts], w_both, start=c == 0, stop=False, skip_group_check=True)
                        for c in range(KC):
                            mm = pe.matmul(both[:, 0:NE], xT_lo[:, c, ts], wr_split[:, c, 0, :], start=False, stop=c == KC - 1,
                                           skip_group_check=True)
                    mm.then_inc(S["bank"], 1)

                def sum_squares():
                    wait(pe, "h_even", f"{NJ - 2}", it)
                    wait(pe, "sumsq", f"{NJ - 1}", it)
                    if it.n == 0:
                        pe.wait_ge(s_ones, 1)
                    for t in range(NT):
                        mm = pe.matmul(A[1][:, t:t + 1], sumsq[:, t * P:(t + 1) * P], ones[:, 0:1].bitcast(F32), start=True, stop=True)
                    mm.then_inc(S["bank"], 1)

                def comb_transposed():
                    wait(pe, "router", "hi2", it)
                    if nxt:
                        wait(pe, "adj", "epsI", it)
                    elif gnn:
                        wait(pe, "h_odd", f"{NJ - 1}", it)
                    else:
                        wait(pe, "router", "copy", it)
                    for t in range(NT):
                        mm = pe.transpose(A[0][0:3 * NE, t * P:(t + 1) * P], comb_stack[:, t, :].bitcast(F32), ident[:, :])
                    mm.then_inc(S["bank"], 1)

                def adj_transposed():
                    loaded(pe, s_adj, it, lambda i: i + 1, per=1)
                    if gnn:
                        wait(pe, "h_odd", f"{NJ - 1}", it)
                    for b in range(GB):
                        mm = pe.transpose(A[0][:, b * P:(b + 1) * P], adj_in[:, b, :], ident[:, :])
                    mm.then_inc(S["bank"], 1)

                def rms_rows():
                    wait(pe, "rms", "diag_lo", it)
                    pe.matmul(A[1][:, :], ones[:, :], diag_hi, start=True, stop=False)
                    pe.matmul(A[1][:, :], ones[:, :], diag_lo, start=False, stop=True).then_inc(S["bank"], 1)

                def b2_rows(y):
                    if y == 0:
                        wait(pe, "router", "combT", it)
                        if it.n == 1:
                            pe.wait_ge(s_eb2, 5)
                    else:
                        wait(pe, "b2", "0", it)
                    for t in range(2):
                        tt = 2 * y + t
                        mm = pe.matmul(A[0][:, t * D:(t + 1) * D], combT[:, tt * P:(tt + 1) * P], eb2_stack[:, :], start=True, stop=True)
                    mm.then_inc(S["bank"], 1)

                def project(j):
                    wait(pe, "act_lo", f"{j}", it)
                    if j == 0:
                        if prev.has("gnn"):
                            wait(pe, "x2", "1", prev)
                        if it.n == 0:
                            pe.wait_ge(s_wlo[1], 1)
                    for y in range(2):
                        for t in range(2):
                            ts = slice((2 * y + t) * P, (2 * y + t + 1) * P)
                            mm = three(O[y][:, t * D:(t + 1) * D], act_hi[:, j % NA, ts], act_lo[:, j % NA, ts],
                                       W2_hi[:, j, :], W2_lo[:, j, :], j == 0 and t == 0, j == NJ - 1)
                    mm.then_inc(S["w2"], 1)

                def aggregate(c):
                    wait(pe, "lo", "xn", it)
                    wait(pe, "adj_lo", "adjT", it)
                    cs = slice(c * P, (c + 1) * P)
                    for g in range(2):
                        if c == 1:
                            wait(pe, "agg_sum", f"0{g}", it)
                        elif g == 0 and moe:
                            wait(pe, "b2", "1", it)
                        elif g == 1 and gnn:
                            wait(pe, "y", f"{NJ - 1}", it)
                        for i in range(2):
                            b = 2 * g + i
                            pe.matmul(A[g][:, 2 * i * N:2 * (i + 1) * N], xn_hi[:, b, cs],
                                      adjT_split[:, b, :, :].rearrange("p s n -> p (s n)"), start=True, stop=False,
                                      skip_group_check=True)
                            mm = pe.matmul(A[g][:, 2 * i * N:(2 * i + 1) * N], xn_lo[:, b, cs], adjT_split[:, b, 0, :],
                                           start=False, stop=True, skip_group_check=True)
                        mm.then_inc(S["bank"], 1)

                def tokens_transposed():
                    for c in range(KC):
                        if nxt:
                            wait(pe, "agg_sum", f"1{c}", it)
                        elif c == 0:
                            if moe:
                                wait(pe, "b2", "1", it)
                        else:
                            wait(pe, "y", f"{NJ - 1}", it)
                        if c == 0:
                            wait(pe, "ln", f"b_x{NT - 1}", it)
                        for t in range(NT):
                            mm = pe.transpose(A[c][:, t * P:(t + 1) * P], xn[:, t, c * P:(c + 1) * P], ident[:, :])
                        mm.then_inc(S["bank"], 1)

                if moe:
                    logits()
                    if it.n == 1:
                        for n in range(2, 2 + NE):
                            pe.wait_ge(s_wlo[n], 1)
                    expert_hidden(0)
                if gnn:
                    for j in range(NJ // 2):
                        hidden_rows(j)
                if moe:
                    expert_hidden(1)
                if gnn:
                    for j in range(NJ // 2, NJ):
                        hidden_rows(j)
                if moe:
                    expert_out(0)
                    expert_hidden(2)
                if nxt:
                    adj_transposed()
                if moe:
                    expert_out(1)
                    expert_hidden(3, (0,))
                if gnn:
                    sum_squares()
                if moe:
                    expert_hidden(3, (1,))
                    expert_out(2)
                if gnn:
                    rms_rows()
                if moe:
                    expert_hidden(4)
                    comb_transposed()
                    expert_out(3)
                if gnn:
                    for j in range(0, 2):
                        project(j)
                if moe:
                    expert_hidden(5)
                if gnn:
                    for j in range(2, 4):
                        project(j)
                if moe:
                    b2_rows(0)
                    expert_out(4)
                if gnn:
                    project(4)
                if moe:
                    expert_hidden(6)
                if moe:
                    b2_rows(1)
                if gnn:
                    for j in range(5, NJ):
                        project(j)
                if nxt:
                    aggregate(0)
                if moe:
                    expert_out(5)
                    expert_hidden(7)
                if nxt:
                    aggregate(1)
                if moe:
                    expert_out(6)
                if gnn:
                    tokens_transposed()
                if moe:
                    expert_out(7)

            body(Step(-1))
            pe.wait_ge(s_small, SMALL)
            pe.transpose(Y[0][:, 0:ROWS], rows, ident[0:ROWS, 0:ROWS]).then_inc(s_turned, 1)
            iterations(pe, body, 0)


_INS = ['x', 'adj', 'L0_gnn_epsilon', 'L0_gnn_W1', 'L0_gnn_b1', 'L0_gnn_rms_weight', 'L0_gnn_W2', 'L0_gnn_b2',
        'L0_ffn_router_w', 'L0_ffn_w1', 'L0_ffn_b1', 'L0_ffn_w2', 'L0_ffn_b2']
_OUTS = [((128, 128, 256), 'float32')]


def kernel(**inputs):
    import numpy as _np
    import concourse.bacc as _bacc
    from concourse import mybir as _mybir
    from concourse.bass_utils import run_bass_kernel_spmd as _run

    nc = _bacc.Bacc("TRN2", target_bir_lowering=False, num_devices=1)
    arrays, args = {}, []
    for name in _INS:
        a = _np.ascontiguousarray(inputs[name])
        if a.ndim == 0:
            a = a.reshape(1)
        arrays[f"in_{name}_dram"] = a
        args.append(nc.dram_tensor(f"in_{name}_dram", a.shape, _mybir.dt.from_np(a.dtype), kind="ExternalInput").ap())
    for i, (shape, dtype) in enumerate(_OUTS):
        dt = _mybir.dt.from_np(_np.dtype(dtype))
        args.append(nc.dram_tensor(f"out_{i}_dram", shape, dt, kind="ExternalOutput").ap())
    gnn_moe_kernel(nc, *args)
    r = _run(nc, [arrays], core_ids=[0])
    got = tuple(r.results[0][f"out_{i}_dram"] for i in range(len(_OUTS)))
    return got[0]
```
